# Optimizing a Trainium2 kernel written in Bass

```python
import numpy as np
import jax
import jax.numpy as jnp

def _softmax(x, axis=-1):
    return jax.nn.softmax(x, axis=axis)

def _gelu(x):
    return jax.nn.gelu(x, approximate=True)

def _silu(x):
    return jax.nn.silu(x)

def _sigmoid(x):
    return jax.nn.sigmoid(x)

def _layernorm(x, axis=-1, eps=1e-05):
    m = jnp.mean(x, axis=axis, keepdims=True)
    v = jnp.var(x, axis=axis, keepdims=True)
    return (x - m) / jnp.sqrt(v + eps)

def _scatter_add(tgt, idx, src, axis=0):
    return tgt.at[idx].add(src)

def _segment_sum(src, seg, n):
    return jax.ops.segment_sum(src, seg, n)
kernel_name = 'mk_xattn_ffn_d1_seqx_r8_21a750'

def setup_inputs(seed: int=0):
    np.random.seed(seed)
    _w = jnp.asarray

    def _rec_inputs():
        import jax
        import jax.numpy as jnp
        _rk = jax.random.key(seed)
        x = 7.22e-05 + 1 * jax.random.normal(jax.random.fold_in(_rk, 1), (16, 128, 256), jnp.float32)
        _lenS = 128 - jax.random.randint(jax.random.fold_in(_rk, 7), (16,), 0, max(1, 128 // 4) + 1, jnp.int32)
        _lenS2 = 128 - jax.random.randint(jax.random.fold_in(_rk, 8), (16,), 0, max(1, 128 // 4) + 1, jnp.int32)
        _ctx_2048P = jax.random.normal(jax.random.fold_in(_rk, 11), (16, 16, 256), jnp.float32)
        _ctx_2048c = jax.random.dirichlet(jax.random.fold_in(_rk, 511), 0.3 * jnp.ones((16,), jnp.float32), (16, 128))
        _ctx_2048t = jnp.einsum('bsk,bkd->bsd', _ctx_2048c, _ctx_2048P)
        _ctx_2048t = _ctx_2048t * jax.lax.rsqrt(jnp.mean(jnp.square(_ctx_2048t)) + 1e-12) * 0.953939
        ctx_2048 = 4.13588e-05 + 0.999923 * (_ctx_2048t + 0.3 * jax.random.normal(jax.random.fold_in(_rk, 611), (16, 128, 256), jnp.float32))
        return (x, ctx_2048)
    x, ctx_2048 = _rec_inputs()

    def _L0_xattn_setup():
        import jax, jax.numpy as jnp
        import numpy as np
        import math
        EMBED = 256
        HEADS = 32
        GROUPS = 8
        GROUP_HEADS = HEADS // GROUPS
        HEAD_DIM = EMBED // HEADS
        B, S = (4, 128)
        key = jax.random.key(seed)
        ks = jax.random.split(key, 8)
        sc = 0.02
        return {'q': jax.random.normal(ks[0], (B, S, EMBED), jnp.float32), 'k': jax.random.normal(ks[1], (B, S, EMBED), jnp.float32), 'v': jax.random.normal(ks[2], (B, S, EMBED), jnp.float32), 'Wq': jax.random.normal(ks[3], (EMBED, EMBED), jnp.float32) * sc, 'Wk': jax.random.normal(ks[4], (GROUPS * HEAD_DIM, EMBED), jnp.float32) * sc, 'Wv': jax.random.normal(ks[5], (GROUPS * HEAD_DIM, EMBED), jnp.float32) * sc, 'Wfc': jax.random.normal(ks[6], (EMBED, EMBED), jnp.float32) * sc, 'bfc': jnp.zeros((EMBED,), jnp.float32)}
    _L0_xattn_all = _L0_xattn_setup()
    _L0_xattn_in = {k: v for k, v in _L0_xattn_all.items() if k in ('Wq', 'Wk', 'Wv', 'Wfc', 'bfc')}
    del _L0_xattn_all

    def _L0_ffn_setup():
        import jax, jax.numpy as jnp
        import numpy as np
        TOP_K = 4
        key = jax.random.key(seed)
        ks = jax.random.split(key, 8)
        B, S, D, E, H, HS = (2, 256, 256, 16, 128, 512)
        scaled = lambda k, shape, fan: jax.random.normal(k, shape, jnp.float32) * fan ** (-0.5)
        return {'x': jax.random.normal(ks[0], (B, S, D), jnp.float32), 'w_router': scaled(ks[1], (D, E), D), 'we1': scaled(ks[2], (E, D, H), D), 'we3': scaled(ks[3], (E, D, H), D), 'we2': scaled(ks[4], (E, H, D), H), 'ws1': scaled(ks[5], (D, HS), D), 'ws3': scaled(ks[6], (D, HS), D), 'ws2': scaled(ks[7], (HS, D), HS)}
    _L0_ffn_all = _L0_ffn_setup()
    _L0_ffn_in = {k: v for k, v in _L0_ffn_all.items() if k in ('w_router', 'we1', 'we3', 'we2', 'ws1', 'ws3', 'ws2')}
    del _L0_ffn_all
    return {'x': x, 'ctx_2048': ctx_2048, 'L0_xattn_Wq': _L0_xattn_in['Wq'], 'L0_xattn_Wk': _L0_xattn_in['Wk'], 'L0_xattn_Wv': _L0_xattn_in['Wv'], 'L0_xattn_Wfc': _L0_xattn_in['Wfc'], 'L0_xattn_bfc': _L0_xattn_in['bfc'], 'L0_ffn_w_router': _L0_ffn_in['w_router'], 'L0_ffn_we1': _L0_ffn_in['we1'], 'L0_ffn_we3': _L0_ffn_in['we3'], 'L0_ffn_we2': _L0_ffn_in['we2'], 'L0_ffn_ws1': _L0_ffn_in['ws1'], 'L0_ffn_ws3': _L0_ffn_in['ws3'], 'L0_ffn_ws2': _L0_ffn_in['ws2']}

def reference(x, ctx_2048, L0_xattn_Wq, L0_xattn_Wk, L0_xattn_Wv, L0_xattn_Wfc, L0_xattn_bfc, L0_ffn_w_router, L0_ffn_we1, L0_ffn_we3, L0_ffn_we2, L0_ffn_ws1, L0_ffn_ws3, L0_ffn_ws2):
    import jax
    import jax.numpy as jnp

    def _L0_xattn_ref(q, k, v, Wq, Wk, Wv, Wfc, bfc):
        import jax, jax.numpy as jnp
        import numpy as np
        import math
        EMBED = 256
        HEADS = 32
        GROUPS = 8
        GROUP_HEADS = HEADS // GROUPS
        HEAD_DIM = EMBED // HEADS
        B, S = (4, 128)
        N, S_, _ = q.shape
        qh = (q @ Wq.T).reshape(N, S_, HEADS, HEAD_DIM).transpose(0, 2, 1, 3)
        kh = (k @ Wk.T).reshape(N, S_, GROUPS, HEAD_DIM).transpose(0, 2, 1, 3)
        vh = (v @ Wv.T).reshape(N, S_, GROUPS, HEAD_DIM).transpose(0, 2, 1, 3)
        kh = jnp.repeat(kh, GROUP_HEADS, axis=1)
        vh = jnp.repeat(vh, GROUP_HEADS, axis=1)
        score = jnp.einsum('bhqd,bhkd->bhqk', qh, kh) / math.sqrt(HEAD_DIM)
        attn = jax.nn.softmax(score, axis=-1)
        out = jnp.einsum('bhqk,bhkd->bhqd', attn, vh)
        out = out.transpose(0, 2, 1, 3).reshape(N, S_, EMBED)
        return out @ Wfc.T + bfc

    def _L0_ffn_ref(x, w_router, we1, we3, we2, ws1, ws3, ws2):
        import jax, jax.numpy as jnp
        import numpy as np
        TOP_K = 4
        B, S, D = x.shape
        T = B * S
        E = w_router.shape[1]
        xt = x.reshape(T, D)
        probs = jax.nn.softmax(xt @ w_router, axis=-1)
        top_w, top_i = jax.lax.top_k(probs, TOP_K)
        top_w = top_w / jnp.sum(top_w, axis=-1, keepdims=True)
        cw = jnp.zeros((T, E), xt.dtype).at[jnp.arange(T)[:, None], top_i].add(top_w)
        g = jax.nn.silu(jnp.einsum('td,edh->teh', xt, we1)) * jnp.einsum('td,edh->teh', xt, we3)
        g = g * cw[:, :, None]
        moe_out = jnp.einsum('teh,ehd->td', g, we2)
        shared = jax.nn.silu(xt @ ws1) * (xt @ ws3) @ ws2
        k = TOP_K
        out = shared / (k + 1) + moe_out * (k / (k + 1))
        return out.reshape(B, S, D)
    x = x + _L0_xattn_ref(_layernorm(x, axis=-1), ctx_2048, ctx_2048, L0_xattn_Wq, L0_xattn_Wk, L0_xattn_Wv, L0_xattn_Wfc, L0_xattn_bfc)
    x = x + _L0_ffn_ref(_layernorm(x, axis=-1), L0_ffn_w_router, L0_ffn_we1, L0_ffn_we3, L0_ffn_we2, L0_ffn_ws1, L0_ffn_ws3, L0_ffn_ws2)
    return x

_drawn_inputs = setup_inputs


def setup_inputs(seed=0):
    import zlib

    import numpy as np

    out = dict(_drawn_inputs(seed))
    spreads = {'L0_xattn_bfc': (0.0, 0.1)}
    factors = {'L0_xattn_Wq': 8.0, 'L0_xattn_Wk': 8.0}
    for name, (base, spread) in spreads.items():
        noise = np.random.default_rng([zlib.crc32(name.encode()), seed]).standard_normal(out[name].shape)
        drawn = base * np.exp(spread * noise) if base else spread * noise
        out[name] = jnp.asarray(drawn.astype(out[name].dtype))
    for name, factor in factors.items():
        out[name] = (out[name] * factor).astype(out[name].dtype)
    return out
```

```python
import concourse.bass as bass
from concourse import mybir
from contextlib import ExitStack

P = 128
D = 256
KC = D // P
NB = 16
S = 128
T = NB * S
HD = 8
GROUPS, GH = 8, 4
HEADS = GROUPS * GH
QUADS = 4
HALVES = GROUPS // QUADS
PARTS = 3
ROWS = PARTS * HD
SCALE = 1.0 / HD ** 0.5
EPS = 1e-5
CH = 512
NC = T // CH
CT = CH // P
E = 16
TOP = 4
SHARED = 4
UNITS = SHARED + E
WU = 3 * D
EARLY = 6
QCOLS = HALVES * GH * S
STACKS = 3
PR = 3
PAIRS = GROUPS // 2
VW = 32
GR = 3
LATE = 2
KROWS = HALVES * QUADS * HD


def build(nc, x, ctxT, WqT, WkT, WvT, WfcT, bfc, wr, W, out):
    f32, f32r, f16, bf16 = mybir.dt.float32, mybir.dt.float32r, mybir.dt.float16, mybir.dt.bfloat16
    ALU, ACT, AX = mybir.AluOpType, mybir.ActivationFunctionType, mybir.AxisListType.X
    q_dram = nc.dram_tensor("q_scratch", [PARTS, NB, QUADS * HD, QCOLS], f32, kind="Internal").ap()
    k_dram = nc.dram_tensor("k_scratch", [PARTS, NB, QUADS * HD, HALVES * S], f32, kind="Internal").ap()
    x_t = x.rearrange("(b p) d -> p b d", p=P)
    out_t = out.rearrange("(b p) d -> p b d", p=P)
    ctx_t = ctxT.rearrange("(k p) t -> p k t", p=P)

    def weight_view(w):
        return w.rearrange("(k p) n -> p k n", p=P)

    with ExitStack() as ctx:
        def sb(name, shape, dt, where=ctx):
            return where.enter_context(nc.sbuf_tensor(name, shape, dt))

        def sem(name):
            return ctx.enter_context(nc.semaphore(name))

        ident = sb("ident", [P, P], f32)
        xres = sb("xres", [P, NB, D], f32)
        stats = sb("stats", [P, NB, 6], f32)
        mv = sb("mv", [P, NB, 2], f32)
        rstd = sb("rstd", [P, NB], f32)
        var = sb("var", [P, NB], f32)
        root = sb("root", [P, NB], f32)
        newton = sb("newton", [P, NB], f32)
        wr_raw = sb("wr_raw", [P, KC, E], f32)
        wr_hi = sb("wr_hi", [P, KC, E], f32r)
        wr_lo = sb("wr_lo", [P, KC, E], f32r)
        raw = [sb(f"raw{i}", [P, WU], f32) for i in range(2)]
        Wu = [sb(f"W{u}", [P, 2, WU], f32r) for u in range(EARLY)]
        att = ExitStack()
        with att:
            wq = sb("wq", [P, KC, D], f32, att)
            wk = sb("wk", [P, KC, KROWS], f32, att)
            wv = sb("wv", [P, KC, GROUPS * HD], f32, att)
            wfc = sb("wfc", [P, KC, D], f32, att)
            bias = sb("bias", [P, D], f32, att)
            cT = sb("cT", [P, KC, T], f32, att)
            xn = sb("xn", [P, CT, D], f32, att)
            xT = sb("xT", [P, KC, CH], f32, att)
            qhl = [sb(f"qhl{c}", [P, HALVES, 2, CH], f32r, att) for c in range(NC)]
            khl = [sb(f"khl{c}", [KROWS, 2, CH], f32r, att) for c in range(NC)]
            vres = sb("vres", [P, CT, GROUPS, HD], f32, att)
            V3 = sb("V3", [P, NB, GROUPS, VW], bf16, att)
            qs = [sb(f"qs{i}", [P, QCOLS], f32r, att) for i in range(STACKS)]
            ks = [sb(f"ks{i}", [P, QUADS, HALVES, S], f32r, att) for i in range(STACKS)]
            zeros = sb("zeros", [QUADS, QCOLS], f32, att)
            p32 = [sb(f"p32_{i}", [P, 2 * GH * S], f32, att) for i in range(PR)]
            phi = [sb(f"phi_{i}", [P, 2 * GH * S], f16, att) for i in range(PR)]
            plo = [sb(f"plo_{i}", [P, 2 * GH * S], f16, att) for i in range(PR)]
            mx = [sb(f"mx{i}", [P, QUADS, HALVES, GH], f32, att) for i in range(STACKS)]
            mrow = [sb(f"mrow{i}", [HEADS, P], f32r, att) for i in range(STACKS)]
            rden = sb("rden", [P, HEADS // 2], f32, att)
            osum = sb("osum", [P, HEADS // 2, HD], f32, att)
            O = sb("O", [P, D], f32, att)
            OT = sb("OT", [P, KC, P], f32, att)
        ex = ExitStack()
        with ex:
            Wu += [sb(f"W{u}", [P, 2, WU], f32r, ex) for u in range(EARLY, UNITS - LATE)]
            x2hi = sb("x2hi", [P, KC, T], f32r, ex)
            x2lo = sb("x2lo", [P, KC, T], f32r, ex)
            cwT = sb("cwT", [2 * E, T], f32r, ex)
            sel = sb("sel", [2 * E, E, P], f32r, ex)
            h = [sb(f"h{i}", [P, CH], f32, ex) for i in range(2)]
            ghi = [sb(f"ghi{i}", [P, CH], f32r, ex) for i in range(GR)]
            glo = [sb(f"glo{i}", [P, CH], f32r, ex) for i in range(GR)]
            router = ExitStack()
            with router:
                xn2 = sb("xn2", [P, CT, D], f32, router)
                lg = sb("lg", [P, NB, E], f32, router)
                pr = sb("pr", [P, NB, E], f32, router)
                above = sb("above", [P, NB, E], f32, router)
                tie = sb("tie", [P, NB, E], f32, router)
                rank = [sb("rank", [P, NB, E], f32, router), lg]
                top8 = sb("top8", [P, NB, 8], f32, router)
                cw = sb("cw", [P, NB, 2, E], f32, router)
                one = sb("one", [P, NB, 1], f32, router)
            Wu += [sb(f"W{u}", [P, 2, WU], f32r, ex) for u in range(UNITS - LATE, UNITS)]

        ysb = [raw[m][:, 0:CH] for m in range(KC)]

        def banks(shapes):
            with ExitStack() as here:
                return [here.enter_context(nc.psum_tensor(name, shape, f32)) for name, shape in shapes]

        psT, psK, psV, *psQ = banks([("psT", [P, KC, CH]), ("psK", [KROWS, CH]), ("psV", [P, 2 * CT, GROUPS * HD]),
                                     ("psQ0", [P, CH]), ("psQ1", [P, CH])])
        psS0, psS1, psST0, psST1, psO, psM = banks([
            ("psS0", [P, GH * S]), ("psS1", [P, GH * S]), ("psST0", [P, 2 * GH * S]), ("psST1", [P, 2 * GH * S]),
            ("psO", [P, HEADS // 2, VW]), ("psM", [P, 2 * D])])
        psS, psST = [psS0, psS1], [psST0, psST1]
        psH0, psH1, psG0, psG1, psC0, psC1, psY0, psY1 = banks([
            (name, [P, CH]) for name in ("psH0", "psH1", "psG0", "psG1", "psC0", "psC1", "psY0", "psY1")])
        psH, psG, psC, psY = [psH0, psH1], [psG0, psG1], [psC0, psC1], [psY0, psY1]
        cwT_banks = [psC1, psY0, psY1, psC0]

        x_in = [sem(f"x_in{c}") for c in range(NC)]
        ctx_in = [sem(f"ctx_in{c}") for c in range(NC)]
        wq_in, wk_in, wv_in, wfc_in, bias_in, wr_in = (sem(n) for n in (
            "wq_in", "wk_in", "wv_in", "wfc_in", "bias_in", "wr_in"))
        raw_in = [sem(f"raw_in{i}") for i in range(2)]
        ident_zero, ident_made, fill_made = sem("ident_zero"), sem("ident_made"), sem("fill_made")
        ks_zero, ks_ready = sem("ks_zero"), sem("ks_ready")
        dve_steps = sem("dve_steps")
        var_made, root_made = sem("var_made"), sem("root_made")
        xn_made, xT_psum, xT_made = sem("xn_made"), sem("xT_psum"), sem("xT_made")
        k_psum, v_psum, q_psum = sem("k_psum"), sem("v_psum"), sem("q_psum")
        hi_made, lo_made, v_made = sem("hi_made"), sem("lo_made"), sem("v_made")
        stacked = [sem(f"stacked{c}") for c in range(NC)]
        stack_in = [sem(f"stack_in{i}") for i in range(STACKS)]
        bias_added = sem("bias_added")
        s_psum, max_made, maxT_psum, row_made = sem("s_psum"), sem("max_made"), sem("maxT_psum"), sem("row_made")
        row_in = [sem(f"row_in{i}") for i in range(STACKS)]
        st_psum, phi_made, p32_made, plo_made = sem("st_psum"), sem("phi_made"), sem("p32_made"), sem("plo_made")
        pv_done, o_read, half_made = sem("pv_done"), sem("o_read"), sem("half_made")
        oT_psum, oT_made, fc_done, x1_made = sem("oT_psum"), sem("oT_made"), sem("fc_done"), sem("x1_made")
        w_hi, w_lo, wr_cut = sem("w_hi"), sem("w_lo"), sem("wr_cut")
        x2_psum, x2_hi_made, x2_lo_made = sem("x2_psum"), sem("x2_hi_made"), sem("x2_lo_made")
        logits, shifted, exps, cw_made = sem("logits"), sem("shifted"), sem("exps"), sem("cw_made")
        cwT_psum, cwT_made, sel_zero, sel_made = sem("cwT_psum"), sem("cwT_made"), sem("sel_zero"), sem("sel_made")
        up_done, gate_done, silu_done, prod_done = sem("up_done"), sem("gate_done"), sem("silu_done"), sem("prod_done")
        ghi_made, glo_made, down_done = sem("ghi_made"), sem("glo_made"), sem("down_done")
        y_made, yT_psum, final, stored = sem("y_made"), sem("yT_psum"), sem("final"), sem("stored")

        class Steps:

            def __init__(self, eng, s):
                self.eng, self.s, self.n = eng, s, 0

            def link(self, ins):
                ins.then_inc(self.s, 1)
                self.n = self.n + 1
                self.eng.wait_ge(self.s, self.n)

        def known(v):
            return isinstance(v, int)

        def wait(eng, s, v):
            if not known(v) or v > 0:
                eng.wait_ge(s, v)

        def batches(eng, body):
            body(0, 0, 0)
            with eng.Fori(0, 4) as i:
                for u in range(1, 4):
                    body(3 * i + u, u % 3, i + u // 3)
            for b in range(13, NB):
                body(b, b % 3, b // 3)

        def first(b):
            return known(b) and b == 0

        def last(b):
            return known(b) and b == NB - 1

        def slot_after(slot, turn):
            return (slot + 1) % STACKS, turn + (slot + 1) // STACKS

        AHEAD = [(0, 1, 2), (3, 4, 5), (6, 7), ()]
        STORES = PARTS * (HALVES * GH + 1)
        STACKED = 16 * STORES
        LOADS = 16 * (2 * QUADS + 1)

        def g_slot_used(n, u):
            return n - (GR - 1) if u >= GR else n - (UNITS % GR) + 1 if u < UNITS % GR else n - (UNITS % GR) - GR + 1

        block = ctx.enter_context(nc.Block())

        @block.sync
        def _(sp):
            for c in range(NC):
                sp.dma_start(xres[:, c * CT:(c + 1) * CT, :], x_t[:, c * CT:(c + 1) * CT, :]).then_inc(x_in[c], 16)

            def load_stack(b, slot):
                for quad in range(QUADS):
                    rows, here = slice(32 * quad, 32 * quad + ROWS), slice(HD * quad, HD * quad + HD)
                    sp.dma_start(qs[slot][rows, :].bitcast(f32),
                                 q_dram[:, bass.ds(b, 1), here, :].rearrange("s b p t -> s (b p) t"))\
                      .then_inc(stack_in[slot], 16)
                    sp.dma_start(ks[slot][rows, quad, :, :].rearrange("p h t -> p (h t)").bitcast(f32),
                                 k_dram[:, bass.ds(b, 1), here, :].rearrange("s b p t -> s (b p) t"))\
                      .then_inc(stack_in[slot], 16)
                sp.dma_start(qs[slot][ROWS:P:32, :].bitcast(f32), zeros[:]).then_inc(stack_in[slot], 16)

            def stores(c):
                bs = slice(c * CT, (c + 1) * CT)
                for part in range(PARTS):
                    q_part, k_part = ((0, 0), (1, 0), (0, 1))[part]
                    for half in range(HALVES):
                        for j in range(GH):
                            at = (half * GH + j) * S
                            yield (q_dram[part, bs, :, at:at + S].rearrange("b p t -> p b t"),
                                   qhl[c][32 * j:32 * j + 32, half, q_part, :])
                    yield (k_dram[part, bs, :, :].rearrange("b p (h t) -> (p h) b t", h=HALVES), khl[c][:, k_part, :])

            def store(c, which):
                for to, src in list(stores(c))[which]:
                    sp.dma_start(to, src.bitcast(f32).rearrange("p (b t) -> p b t", b=CT)).then_inc(stacked[c], 16)

            for c in range(2):
                sp.wait_ge(hi_made, 3 * (c + 1))
                sp.wait_ge(lo_made, 3 * (c + 1))
                store(c, slice(0, STORES))
                if c == 0:
                    sp.wait_ge(stacked[0], STACKED)
                    sp.wait_ge(fill_made, 2)
                    sp.wait_ge(ks_ready, STACKS)
                    for b in range(STACKS):
                        load_stack(b, b)

            def sp_batch(b, slot, turn):
                sp.wait_ge(row_made, b + 1)
                sp.dma_start(qs[slot][ROWS:P:32, :].bitcast(f32), mrow[slot][:].bitcast(f32)).then_inc(row_in[slot], 16)
                if known(b) and b < 2 * STACKS:
                    c, third = 2 + b // 3, STORES // 3
                    if b % 3 == 0:
                        sp.wait_ge(hi_made, 3 * (c + 1))
                        sp.wait_ge(lo_made, 3 * (c + 1))
                    store(c, slice(b % 3 * third, (b % 3 + 1) * third))
                if not first(b) and not (known(b) and b + 2 >= NB):
                    if known(b) and b < 7 and (b + 2) % CT == 0:
                        sp.wait_ge(stacked[(b + 2) // CT], STACKED)
                    sp.wait_ge(st_psum, PAIRS * b)
                    load_stack(b + 2, (slot + 2) % STACKS)

            for b in range(7):
                sp_batch(b, b % 3, b // 3)
            sp.wait_ge(stacked[3], STACKED)
            with sp.Fori(2, 4) as i:
                for u in range(1, 4):
                    sp_batch(3 * i + u, u % 3, i + u // 3)
            for b in range(13, NB):
                sp_batch(b, b % 3, b // 3)
            for c in range(NC):
                sp.wait_ge(final, 2 * (c + 1))
                sp.dma_start(out_t[:, c * CT:(c + 1) * CT, :], xres[:, c * CT:(c + 1) * CT, :]).then_inc(stored, 16)
            sp.wait_ge(stored, 16 * NC)

        @block.scalar
        def _(act):
            act.dma_start(wk[:], weight_view(WkT)).then_inc(wk_in, 16)
            act.dma_start(cT[:, :, 0:CH], ctx_t[:, :, 0:CH]).then_inc(ctx_in[0], 16)
            act.dma_start(wv[:], weight_view(WvT)).then_inc(wv_in, 16)
            act.dma_start(wq[:], weight_view(WqT)).then_inc(wq_in, 16)
            for c in range(1, NC):
                act.dma_start(cT[:, :, c * CH:(c + 1) * CH], ctx_t[:, :, c * CH:(c + 1) * CH]).then_inc(ctx_in[c], 16)
            act.dma_start(bias[:], bfc.partition_broadcast(P)).then_inc(bias_in, 16)
            act.dma_start(wfc[:], weight_view(WfcT)).then_inc(wfc_in, 16)
            act.dma_start(wr_raw[:], weight_view(wr)).then_inc(wr_in, 16)

            act.wait_ge(var_made, 1)
            act.activation(root[:], var[:], ACT.Sqrt).then_inc(root_made, 1)
            for c in range(NC):
                act.wait_ge(xT_psum, c + 1)
                wait(act, q_psum, 2 * c)
                act.activation(xT[:], psT[:], ACT.Copy).then_inc(xT_made, 1)
                act.wait_ge(k_psum, c + 1)
                act.activation(khl[c][:, 0, :], psK[:], ACT.Copy).then_inc(hi_made, 1)
                for half in range(HALVES):
                    act.wait_ge(q_psum, 2 * c + half + 1)
                    act.activation(qhl[c][:, half, 0, :], psQ[half][:], ACT.Copy).then_inc(hi_made, 1)

            def act_oT(b):
                act.wait_ge(oT_psum, b + 1)
                act.activation(OT[:].rearrange("p k t -> p (k t)"), psM[:, 0:D], ACT.Copy).then_inc(oT_made, 1)

            def act_batch(b, slot, turn):
                for p in range(PAIRS):
                    n, r = PAIRS * b + p, (slot + p) % PR
                    if p == 3 and not first(b):
                        act_oT(b - 1)
                    act.wait_ge(st_psum, n + 1)
                    wait(act, pv_done, n - PR + 1)
                    act.activation(phi[r][:], psST[p % 2][:], ACT.Exp, scale=SCALE).then_inc(phi_made, 1)
                    wait(act, plo_made, n - PR + 1)
                    act.activation(p32[r][:], psST[p % 2][:], ACT.Exp, scale=SCALE).then_inc(p32_made, 1)

            batches(act, act_batch)
            act_oT(NB - 1)

            act.wait_ge(var_made, 2)
            act.activation(root[:], var[:], ACT.Sqrt).then_inc(root_made, 1)
            for c in range(NC):
                act.wait_ge(x2_psum, c + 1)
                for k in range(KC):
                    act.activation(x2hi[:, k, c * CH:(c + 1) * CH], (psH, psG)[c % 2][k][:], ACT.Copy)\
                       .then_inc(x2_hi_made, 1)
            act.wait_ge(shifted, 1)
            act.activation(pr[:], lg[:], ACT.Exp).then_inc(exps, 1)
            for c in range(NC):
                act.wait_ge(cwT_psum, c + 1)
                act.activation(cwT[:, c * CH:(c + 1) * CH], cwT_banks[c][0:2 * E, :], ACT.Copy).then_inc(cwT_made, 1)

            def act_y(c):
                act.wait_ge(down_done, UNITS * (c + 1))
                wait(act, yT_psum, c)
                for m in range(KC):
                    act.activation(ysb[m], psY[m][:], ACT.Copy).then_inc(y_made, 1)

            def act_chunk(c):
                for u in range(UNITS):
                    n = UNITS * c + u
                    act.wait_ge(up_done, n + 1)
                    wait(act, glo_made, n - 1)
                    act.activation(h[u % 2][:], psH[u % 2][:], ACT.Silu).then_inc(silu_done, 1)
                    act.wait_ge(prod_done, n + 1)
                    wait(act, down_done, g_slot_used(n, u))
                    act.activation(ghi[u % GR][:], h[u % 2][:], ACT.Copy).then_inc(ghi_made, 1)
                    if u == 1 and not first(c):
                        act_y(c - 1)

            act_chunk(0)
            with act.Fori(1, NC) as c:
                act_chunk(c)
            act_y(NC - 1)

        @block.gpsimd
        def _(pool):
            pool.memset(ident[:], 0.0).then_inc(ident_zero, 1)
            pool.wait_ge(ident_zero, 1)
            pool.affine_select(out=ident[:], in_=ident[:], compare_op=ALU.not_equal, fill=1.0, base=0,
                               pattern=[[-1, P]], channel_multiplier=1).then_inc(ident_made, 1)

            def load_raw(u):
                wait(pool, w_lo, u - 1)
                pool.dma_start(raw[u % 2][:], W[u]).then_inc(raw_in[u % 2], 16)

            def cut_lo(u):
                pool.wait_ge(w_hi, u + 1)
                pool.tensor_tensor(Wu[u][:, 1, :], raw[u % 2][:], Wu[u][:, 0, :].bitcast(f32), ALU.subtract)\
                    .then_inc(w_lo, 1)
                if u + 2 < UNITS:
                    load_raw(u + 2)

            load_raw(0)
            load_raw(1)
            for slot in range(STACKS):
                pool.wait_ge(ks_zero, 1)
                pool.affine_select(out=ks[slot][:].rearrange("p q h t -> p q (h t)"),
                                   in_=ks[slot][:].rearrange("p q h t -> p q (h t)").bitcast(f32),
                                   compare_op=ALU.not_equal, fill=-1.0, base=-ROWS,
                                   pattern=[[-32, QUADS], [0, HALVES * S]], channel_multiplier=1).then_inc(ks_ready, 1)
            for u in range(EARLY):
                cut_lo(u)
            pool.wait_ge(bias_in, 16)
            for c in range(NC):
                pool.wait_ge(xn_made, CT * (c + 1))
                here = xres[:, c * CT:(c + 1) * CT, :]
                pool.tensor_tensor(here, here, bias[:].unsqueeze(1).broadcast_to([P, CT, D]), ALU.add)\
                    .then_inc(bias_added, 1)

            def pool_batch(b, slot, turn):
                for p in range(PAIRS):
                    n, r = PAIRS * b + p, (slot + p) % PR
                    pool.wait_ge(p32_made, n + 1)
                    wait(pool, pv_done, n - PR + 1)
                    pool.tensor_tensor(plo[r][:], p32[r][:], phi[r][:], ALU.subtract).then_inc(plo_made, 1)

            batches(pool, pool_batch)

            pool.wait_ge(x1_made, NB)
            pool.memset(sel[:].bitcast(f32), 0.0).then_inc(sel_zero, 1)
            for part in range(2):
                pool.wait_ge(sel_zero, part + 1)
                pool.affine_select(out=sel[:], in_=sel[:].bitcast(f32), compare_op=ALU.not_equal, fill=1.0,
                                   base=-E * part, pattern=[[-1, E], [0, P]], channel_multiplier=1)\
                    .then_inc(sel_zero if part == 0 else sel_made, 1)
            for u in range(EARLY, UNITS):
                cut_lo(u)

        @block.vector
        def _(dve):
            steps = Steps(dve, dve_steps)

            def make_rstd(times):
                steps.link(dve.tensor_scalar(var[:], mv[:, :, 1], EPS, None, ALU.add))
                dve.tensor_copy(newton[:], var[:]).then_inc(var_made, 1)
                dve.wait_ge(root_made, times)
                steps.link(dve.reciprocal(rstd[:], root[:]))
                steps.link(dve.tensor_tensor(newton[:], rstd[:], rstd[:], ALU.mult))
                steps.link(dve.tensor_tensor(newton[:], newton[:], var[:], ALU.mult))
                steps.link(dve.tensor_scalar(newton[:], newton[:], -0.5, 1.5, ALU.mult, ALU.add))
                steps.link(dve.tensor_tensor(rstd[:], rstd[:], newton[:], ALU.mult))

            def cut_hi(u):
                dve.wait_ge(raw_in[u % 2], 16 * (u // 2 + 1))
                dve.tensor_copy(Wu[u][:, 0, :], raw[u % 2][:]).then_inc(w_hi, 1)

            def normed(to, b):
                return dve.tensor_scalar(to, xres[:, b, :], mv[:, b, 0:1], rstd[:, b:b + 1], ALU.subtract, ALU.mult)

            for slot in range(STACKS):
                ins = dve.memset(ks[slot][:].bitcast(f32), 0.0)
            ins.then_inc(ks_zero, 1)
            for b in range(NB):
                if b % CT == 0:
                    dve.wait_ge(x_in[b // CT], 16)
                ins = dve.bn_stats(stats[:, b, :], xres[:, b, :])
            steps.link(ins)
            for b in range(NB):
                ins = dve.bn_aggr(mv[:, b, :], stats[:, b, :])
            steps.link(ins)
            make_rstd(1)
            for slot in range(STACKS):
                dve.memset(qs[slot][:].bitcast(f32), 0.0)
            dve.memset(zeros[:], 0.0).then_inc(fill_made, 1)
            dve.memset(V3[:], 1.0).then_inc(fill_made, 1)
            dve.wait_ge(fill_made, 2)
            cut_hi(0)
            cut_hi(1)
            for c in range(NC):
                for t in range(CT):
                    if t == 0:
                        wait(dve, xT_psum, c)
                    normed(xn[:, t, :], c * CT + t).then_inc(xn_made, 1)
                dve.wait_ge(v_psum, c + 1)
                vps = psV[:, 0:CT, :].rearrange("p t (g d) -> p t g d", g=GROUPS)
                part = [V3[:, c * CT:(c + 1) * CT, :, HD * i:HD * (i + 1)] for i in range(3)]
                steps.link(dve.tensor_copy(part[0], vps))
                steps.link(dve.tensor_tensor(vres[:], vps, part[0], ALU.subtract))
                steps.link(dve.tensor_copy(part[1], vres[:]))
                steps.link(dve.tensor_tensor(vres[:], vres[:], part[1], ALU.subtract))
                dve.tensor_copy(part[2], vres[:]).then_inc(v_made, 1)
                dve.wait_ge(hi_made, 3 * c + 1)
                dve.tensor_tensor(khl[c][:, 1, :], psK[:], khl[c][:, 0, :].bitcast(f32), ALU.subtract)\
                   .then_inc(lo_made, 1)
                for half in range(HALVES):
                    dve.wait_ge(hi_made, 3 * c + half + 2)
                    dve.tensor_tensor(qhl[c][:, half, 1, :], psQ[half][:], qhl[c][:, half, 0, :].bitcast(f32),
                                      ALU.subtract).then_inc(lo_made, 1)
                cut_hi(2 + c)
            for u in range(2 + NC, EARLY):
                cut_hi(u)

            def maximum(b, g, slot):
                dve.wait_ge(s_psum, GROUPS * b + g + 1)
                if g == 0:
                    wait(dve, maxT_psum, b - STACKS + 1)
                dve.tensor_reduce(mx[slot][:, :, g // GH, g % GH], psS[g % 2][:].rearrange("p (q t) -> p q t", q=QUADS),
                                  AX, ALU.max).then_inc(max_made, 1)

            def max_row(b, slot):
                dve.wait_ge(maxT_psum, b + 1)
                dve.tensor_copy(mrow[slot][:], psM[0:HEADS, 0:P]).then_inc(row_made, 1)

            def combine(b, half):
                dve.wait_ge(pv_done, PAIRS * b + 2 * half + 2)
                wait(dve, half_made, 2 * b + half)
                dve.reciprocal(rden[:], psO[:, :, 3 * HD])
                dve.tensor_reduce(osum[:], psO[:, :, 0:3 * HD].rearrange("p h (s d) -> p h d s", s=3), AX, ALU.add)\
                   .then_inc(o_read, 1)
                dve.wait_ge(o_read, 2 * b + half + 1)
                if half == 0:
                    wait(dve, oT_psum, b)
                dve.tensor_tensor(O[:, half * P:(half + 1) * P].rearrange("p (h d) -> p h d", d=HD), osum[:],
                                  rden[:].unsqueeze(2).broadcast_to([P, HEADS // 2, HD]), ALU.mult)\
                   .then_inc(half_made, 1)

            def residual(b):
                dve.wait_ge(fc_done, b + 1)
                here = xres[:, bass.ds(b, 1), :].rearrange("p b d -> p (b d)")
                dve.tensor_tensor(here, psM[:, D:2 * D], here, ALU.add).then_inc(x1_made, 1)
                dve.wait_ge(x1_made, b + 1)
                dve.bn_stats(stats[:, bass.ds(b, 1), :].rearrange("p b s -> p (b s)"), here)

            def dve_batch(b, slot, turn):
                nslot, _ = slot_after(slot, turn)
                if not last(b):
                    for p in range(PAIRS):
                        for g in AHEAD[p]:
                            maximum(b + 1, g, nslot)
                    max_row(b + 1, nslot)
                if not first(b):
                    combine(b - 1, 1)
                    residual(b - 1)
                combine(b, 0)

            for g in range(GROUPS):
                maximum(0, g, 0)
            max_row(0, 0)
            dve.wait_ge(bias_added, NC)
            batches(dve, dve_batch)
            combine(NB - 1, 1)
            residual(NB - 1)
            steps.link(dve.tensor_copy(newton[:], rstd[:]))
            for b in range(NB):
                ins = dve.bn_aggr(mv[:, b, :], stats[:, b, :])
            steps.link(ins)
            make_rstd(2)
            for c in range(NC):
                for t in range(CT):
                    if t == 0:
                        wait(dve, x2_psum, c)
                    normed(xn2[:, t, :], c * CT + t).then_inc(xn_made, 1)
                if c == 0:
                    dve.wait_ge(wr_in, 16)
                    steps.link(dve.tensor_copy(wr_hi[:], wr_raw[:]))
                    dve.tensor_tensor(wr_lo[:], wr_raw[:], wr_hi[:].bitcast(f32), ALU.subtract).then_inc(wr_cut, 1)
                for k in range(KC):
                    dve.wait_ge(x2_hi_made, KC * c + k + 1)
                    here = slice(c * CH, (c + 1) * CH)
                    dve.tensor_tensor(x2lo[:, k, here], (psH, psG)[c % 2][k][:], x2hi[:, k, here].bitcast(f32),
                                      ALU.subtract).then_inc(x2_lo_made, 1)
            dve.wait_ge(logits, 1)
            lps = psC[0][:, 0:NB * E].rearrange("p (b e) -> p b e", e=E)
            per_expert = [P, NB, E]
            steps.link(dve.tensor_reduce(one[:, :, 0], lps, AX, ALU.max))
            dve.tensor_tensor(lg[:], lps, one[:].broadcast_to(per_expert), ALU.subtract).then_inc(shifted, 1)
            dve.wait_ge(exps, 1)
            steps.link(dve.tensor_reduce(one[:, :, 0], pr[:], AX, ALU.add))
            steps.link(dve.reciprocal(one[:], one[:]))
            steps.link(dve.tensor_tensor(pr[:], pr[:], one[:].broadcast_to(per_expert), ALU.mult))
            for b in range(NB):
                ins = dve.max(top8[:, b, :], pr[:, b, :])
            steps.link(ins)
            fourth = top8[:, :, TOP - 1:TOP].broadcast_to(per_expert)
            dve.tensor_tensor(above[:], pr[:], fourth, ALU.is_gt)
            steps.link(dve.tensor_tensor(tie[:], pr[:], fourth, ALU.is_equal))
            steps.link(dve.tensor_reduce(one[:, :, 0], above[:], AX, ALU.add))
            src = tie
            for i in range(4):
                dst, step = rank[i % 2], 1 << i
                dve.tensor_copy(dst[:, :, 0:step], src[:, :, 0:step])
                steps.link(dve.tensor_tensor(dst[:, :, step:], src[:, :, step:], src[:, :, 0:E - step], ALU.add))
                src = dst
            steps.link(dve.tensor_tensor(rank[0][:], src[:], one[:].broadcast_to(per_expert), ALU.add))
            steps.link(dve.scalar_tensor_tensor(rank[1][:], rank[0][:], float(TOP), tie[:], ALU.is_le, ALU.mult))
            steps.link(dve.tensor_tensor(rank[0][:], rank[1][:], above[:], ALU.add))
            steps.link(dve.tensor_tensor(lg[:], rank[0][:], pr[:], ALU.mult))
            steps.link(dve.tensor_reduce(one[:, :, 0], lg[:], AX, ALU.add))
            steps.link(dve.reciprocal(one[:], one[:]))
            steps.link(dve.tensor_scalar(one[:], one[:], TOP / (TOP + 1.0), None, ALU.mult))
            steps.link(dve.tensor_tensor(lg[:], lg[:], one[:].broadcast_to(per_expert), ALU.mult))
            steps.link(dve.tensor_copy(cw[:, :, 0, :].bitcast(f32r), lg[:]))
            dve.tensor_tensor(cw[:, :, 1, :].bitcast(f32r), lg[:], cw[:, :, 0, :], ALU.subtract).then_inc(cw_made, 1)

            def add_y(c):
                dve.wait_ge(yT_psum, c + 1)
                for i in range(2):
                    here = xres[:, bass.ds(c * CT + 2 * i, 2), :].rearrange("p b d -> p (b d)")
                    dve.tensor_tensor(here, psC[i][:], here, ALU.add).then_inc(final, 1)

            def dve_unit(n, u):
                hu, weights = h[u % 2][:], psC[u % 2][:]
                dve.wait_ge(silu_done, n + 1)
                dve.wait_ge(gate_done, n + 1)
                if u < SHARED:
                    dve.scalar_tensor_tensor(hu, hu, 1.0 / (TOP + 1), psG[u % 2][:], ALU.mult, ALU.mult)\
                       .then_inc(prod_done, 1)
                else:
                    steps.link(dve.tensor_tensor(hu, hu, psG[u % 2][:], ALU.mult))
                    dve.tensor_tensor(hu, hu, weights, ALU.mult).then_inc(prod_done, 1)
                dve.wait_ge(ghi_made, n + 1)
                wait(dve, down_done, g_slot_used(n, u))
                dve.tensor_tensor(glo[u % GR][:], hu, ghi[u % GR][:].bitcast(f32), ALU.subtract).then_inc(glo_made, 1)

            for u in range(UNITS):
                dve_unit(u, u)
                if EARLY + u < UNITS:
                    if EARLY + u >= UNITS - LATE:
                        dve.wait_ge(cwT_psum, NC)
                    cut_hi(EARLY + u)
            base = steps.n
            with dve.Fori(1, NC) as c:
                steps.n = base + E * (c - 1)
                for u in range(UNITS):
                    dve_unit(UNITS * c + u, u)
                    if u == 3:
                        add_y(c - 1)
            add_y(NC - 1)

        @block.tensor
        def _(pe):
            mm = pe.matmul

            pe.wait_ge(ident_made, 1)
            for c in range(NC):
                cs = c * CH
                if c == 0:
                    pe.wait_ge(wk_in, 16)
                pe.wait_ge(ctx_in[c], 16)
                wait(pe, lo_made, 3 * c - 2)
                for k in range(KC):
                    ins = mm(psK[:], wk[:, k, :], cT[:, k, cs:cs + CH], start=k == 0, stop=k == KC - 1)
                ins.then_inc(k_psum, 1)
                if c == 0:
                    pe.wait_ge(wv_in, 16)
                wait(pe, v_made, c)
                for t in range(CT):
                    for k in range(KC):
                        ins = mm(psV[:, t, :], cT[:, k, cs + t * P:cs + (t + 1) * P], wv[:, k, :],
                                 start=k == 0, stop=k == KC - 1)
                ins.then_inc(v_psum, 1)
                wait(pe, xT_made, c)
                for t in range(CT):
                    pe.wait_ge(xn_made, c * CT + t + 1)
                    for k in range(KC):
                        ins = pe.transpose(psT[:, k, t * P:(t + 1) * P], xn[:, t, k * P:(k + 1) * P], ident[:])
                ins.then_inc(xT_psum, 1)
                if c == 0:
                    pe.wait_ge(wq_in, 16)
                pe.wait_ge(xT_made, c + 1)
                for half in range(HALVES):
                    wait(pe, lo_made, 3 * (c - 1) + half + 2)
                    for k in range(KC):
                        ins = mm(psQ[half][:], wq[:, k, half * P:(half + 1) * P], xT[:, k, :],
                                 start=k == 0, stop=k == KC - 1)
                    ins.then_inc(q_psum, 1)

            def scores(b, g, slot, turn):
                if g == 0:
                    pe.wait_ge(stack_in[slot], LOADS * (turn + 1))
                wait(pe, max_made, GROUPS * b + g - 1)
                ins = mm(psS[g % 2][:], qs[slot][:, g * S:(g + 1) * S], ks[slot][:, :, g // GH, :], start=True, stop=True)
                ins.then_inc(s_psum, 1)

            def maxima_T(b, slot):
                pe.wait_ge(max_made, GROUPS * (b + 1))
                wait(pe, x1_made, b - 2)
                pe.transpose(psM[0:HEADS, 0:P], mx[slot][:].rearrange("p q h j -> p (q h j)"), ident[:]).then_inc(maxT_psum, 1)

            def scores_T(b, p, slot, turn):
                wait(pe, p32_made, PAIRS * b + p - 1)
                if p == 0:
                    pe.wait_ge(row_in[slot], 16 * (turn + 1))
                for i in range(2):
                    g = 2 * p + i
                    half = g // QUADS
                    ins = mm(psST[p % 2][:, i * GH * S:(i + 1) * GH * S], ks[slot][:, g % QUADS, half, :],
                             qs[slot][:, half * GH * S:(half + 1) * GH * S], start=True, stop=True)
                ins.then_inc(st_psum, 1)

            def values(b, p, slot):
                r = (slot + p) % PR
                if p % 2 == 0:
                    wait(pe, o_read, 2 * b + p // 2)
                pe.wait_ge(phi_made, PAIRS * b + p + 1)
                pe.wait_ge(plo_made, PAIRS * b + p + 1)
                for i in range(2 * GH):
                    g = 2 * p + i // GH
                    v = V3[:, bass.ds(b, 1), g, 0:3 * HD + 1].rearrange("p b d -> p (b d)")
                    to = psO[:, (p % 2) * 2 * GH + i, 0:3 * HD + 1]
                    mm(to, phi[r][:, i * S:(i + 1) * S], v, start=True, stop=False)
                    ins = mm(to, plo[r][:, i * S:(i + 1) * S], v, start=False, stop=True)
                ins.then_inc(pv_done, 1)

            def transpose_O(b):
                pe.wait_ge(half_made, 2 * (b + 1))
                pe.wait_ge(row_made, min(b + 3, NB) if known(b) else b + 3)
                wait(pe, x1_made, b)
                for k in range(KC):
                    ins = pe.transpose(psM[:, k * P:(k + 1) * P], O[:, k * P:(k + 1) * P], ident[:])
                ins.then_inc(oT_psum, 1)

            def project(b):
                pe.wait_ge(oT_made, b + 1)
                for k in range(KC):
                    ins = mm(psM[:, D:2 * D], OT[:, k, :], wfc[:, k, :], start=k == 0, stop=k == KC - 1)
                ins.then_inc(fc_done, 1)

            def pe_batch(b, slot, turn):
                nslot, nturn = slot_after(slot, turn)
                before = (slot + STACKS - 1) % STACKS
                for p in range(PAIRS):
                    if p == 3 and not first(b):
                        transpose_O(b - 1)
                    scores_T(b, p, slot, turn)
                    if not last(b):
                        for g in AHEAD[p]:
                            scores(b + 1, g, nslot, nturn)
                    if p == 2 and not last(b):
                        maxima_T(b + 1, nslot)
                    if p >= 2:
                        values(b, p - 2, slot)
                    elif not first(b):
                        values(b - 1, p + 2, before)
                if not first(b):
                    project(b - 1)

            pe.wait_ge(xT_made, NC)
            pe.wait_ge(v_made, NC)
            pe.wait_ge(lo_made, 3 * NC)
            for g in range(GROUPS):
                scores(0, g, 0, 0)
            maxima_T(0, 0)
            pe.wait_ge(wfc_in, 16)
            batches(pe, pe_batch)
            for p in (2, 3):
                values(NB - 1, p, (NB - 1) % STACKS)
            transpose_O(NB - 1)
            project(NB - 1)

            for c in range(NC):
                wait(pe, x2_lo_made, KC * (c - 1))
                for t in range(CT):
                    pe.wait_ge(xn_made, NB + c * CT + t + 1)
                    for k in range(KC):
                        ins = pe.transpose((psH, psG)[c % 2][k][:, t * P:(t + 1) * P],
                                           xn2[:, t, k * P:(k + 1) * P], ident[:])
                ins.then_inc(x2_psum, 1)
            pe.wait_ge(wr_cut, 1)
            for c in range(NC):
                pe.wait_ge(x2_lo_made, KC * (c + 1))
                for b in range(c * CT, (c + 1) * CT):
                    to = psC[0][:, b * E:(b + 1) * E]
                    i = 0
                    for k in range(KC):
                        for xs, ws in ((x2hi, wr_hi), (x2hi, wr_lo), (x2lo, wr_hi)):
                            ins = mm(to, xs[:, k, b * P:(b + 1) * P], ws[:, k, :], start=i == 0, stop=i == 5)
                            i += 1
            ins.then_inc(logits, 1)

            def cut_products(to, w, col, c):
                i = 0
                for k in range(KC):
                    at = w[:, 0, col + k * P:col + (k + 1) * P], w[:, 1, col + k * P:col + (k + 1) * P]
                    for ws, xv in ((at[0], x2hi), (at[1], x2hi), (at[0], x2lo)):
                        ins = mm(to, ws, xv[:, k, bass.ds(c * CH, CH)], start=i == 0, stop=i == 3 * KC - 1)
                        i += 1
                return ins

            def up(c, u):
                n = UNITS * c + u
                pe.wait_ge(w_lo, u + 1)
                wait(pe, silu_done, n - 1)
                cut_products(psH[u % 2][:], Wu[u], 0, c).then_inc(up_done, 1)
                wait(pe, prod_done, n - 1)
                if SHARED <= u < SHARED + 2 and not first(c):
                    pe.wait_ge(final, 2 * c)
                ins = cut_products(psG[u % 2][:], Wu[u], D, c)
                if u >= SHARED:
                    ins = mm(psC[u % 2][:], sel[:, u - SHARED, :], cwT[:, bass.ds(c * CH, CH)], start=True, stop=True)
                ins.then_inc(gate_done, 1)

            def down(c, u):
                if u == 0:
                    wait(pe, y_made, KC * c)
                pe.wait_ge(glo_made, UNITS * c + u + 1)
                for m in range(KC):
                    at = 2 * D + m * P
                    i = 0
                    for wp, gs in ((0, ghi), (1, ghi), (0, glo)):
                        ins = mm(psY[m][:], Wu[u][:, wp, at:at + P], gs[u % GR][:], start=u == 0 and i == 0,
                                 stop=u == UNITS - 1 and i == 2)
                        i += 1
                ins.then_inc(down_done, 1)

            def transpose_y(c):
                pe.wait_ge(y_made, KC * (c + 1))
                pe.wait_ge(prod_done, UNITS * (c + 1))
                for t in range(CT):
                    for m in range(KC):
                        ins = pe.transpose(psC[t // 2][:, ((t % 2) * KC + m) * P:((t % 2) * KC + m + 1) * P],
                                           ysb[m][:, t * P:(t + 1) * P], ident[:])
                ins.then_inc(yT_psum, 1)

            def pe_chunk(c):
                for u in range(UNITS):
                    if u == SHARED and first(c):
                        pe.wait_ge(sel_made, 1)
                    if u == 2 and first(c):
                        weights_T()
                    up(c, u)
                    if u < 2:
                        if not first(c):
                            down(c - 1, UNITS - 2 + u)
                    else:
                        if u == 2 and not first(c):
                            transpose_y(c - 1)
                        down(c, u - 2)

            def weights_T():
                pe.wait_ge(cw_made, 1)
                for c in range(NC):
                    for t in range(CT):
                        ins = pe.transpose(cwT_banks[c][0:2 * E, t * P:(t + 1) * P],
                                           cw[:, c * CT + t, :, :].rearrange("p a e -> p (a e)"), ident[:])
                    ins.then_inc(cwT_psum, 1)
                pe.wait_ge(cwT_made, NC)

            pe_chunk(0)
            with pe.Fori(1, NC) as c:
                pe_chunk(c)
            down(NC - 1, UNITS - 2)
            down(NC - 1, UNITS - 1)
            transpose_y(NC - 1)


def kernel(x, ctx_2048, L0_xattn_Wq, L0_xattn_Wk, L0_xattn_Wv, L0_xattn_Wfc, L0_xattn_bfc, L0_ffn_w_router,
           L0_ffn_we1, L0_ffn_we3, L0_ffn_we2, L0_ffn_ws1, L0_ffn_ws3, L0_ffn_ws2):
    import numpy as np
    import concourse.bacc as bacc
    from concourse.bass_utils import run_bass_kernel_spmd

    def halves_of(w):
        return np.concatenate([w[..., k * P:(k + 1) * P, :] for k in range(KC)], axis=-1)

    def columns(w):
        return np.stack([w[:, u * P:(u + 1) * P] for u in range(SHARED)])

    a = {k: np.asarray(v) for k, v in dict(
        x=x, ctx=ctx_2048, Wq=L0_xattn_Wq, Wk=L0_xattn_Wk, Wv=L0_xattn_Wv, Wfc=L0_xattn_Wfc, bfc=L0_xattn_bfc,
        wr=L0_ffn_w_router, we1=L0_ffn_we1, we3=L0_ffn_we3, we2=L0_ffn_we2, ws1=L0_ffn_ws1, ws3=L0_ffn_ws3,
        ws2=L0_ffn_ws2).items()}
    wq = a["Wq"].reshape(HALVES, QUADS, GH, HD, D).transpose(0, 2, 1, 3, 4).reshape(D, D)
    shared = np.concatenate([halves_of(columns(a["ws1"])), halves_of(columns(a["ws3"])),
                             a["ws2"].reshape(SHARED, P, D)], axis=-1)
    experts = np.concatenate([halves_of(a["we1"]), halves_of(a["we3"]), a["we2"]], axis=-1)
    wk = a["Wk"].reshape(HALVES, QUADS, HD, D).transpose(1, 2, 0, 3).reshape(KROWS, D)
    arrays = {
        "x": a["x"].reshape(T, D), "ctxT": a["ctx"].reshape(T, D).T, "WqT": wq.T, "WkT": wk.T, "WvT": a["Wv"].T,
        "WfcT": a["Wfc"].T, "bfc": a["bfc"], "wr": a["wr"], "W": np.concatenate([shared, experts]),
    }
    nc = bacc.Bacc("TRN2", target_bir_lowering=False, num_devices=1)
    args, given = {}, {}
    for name, v in arrays.items():
        v = np.ascontiguousarray(v)
        given[f"in_{name}"] = v
        args[name] = nc.dram_tensor(f"in_{name}", v.shape, mybir.dt.from_np(v.dtype), kind="ExternalInput").ap()
    out = nc.dram_tensor("out_0", (T, D), mybir.dt.float32, kind="ExternalOutput").ap()
    build(nc, out=out, **args)
    got = run_bass_kernel_spmd(nc, [given], core_ids=[0])
    return got.results[0]["out_0"].reshape(NB, S, D)
```

```python
import concourse.bass as bass
from concourse import mybir
from contextlib import ExitStack

P = 128
D = 256
KC = D // P
NB = 16
S = 128
T = NB * S
HD = 8
GROUPS, GH = 8, 4
HEADS = GROUPS * GH
QUADS = 4
HALVES = GROUPS // QUADS
PARTS = 3
GROUP_ROWS = QUADS * HD
ROWS = PARTS * GROUP_ROWS
SCALE = 1.0 / HD ** 0.5
EPS = 1e-5
CH = 512
NC = T // CH
CT = CH // P
E = 16
TOP = 4
SHARED = 4
UNITS = SHARED + E
WU = 3 * D
EARLY = 6
QCOLS = HALVES * GH * S
STACKS = 4
PAIRS = GROUPS // 2
PR = PAIRS
QR = 2
VW = 32
GR = 3
LATE = 2


def build(nc, x, ctxT, WqT, WkT, WvT, WfcT, bfc, wr, W, out):
    f32, f32r, f16, bf16 = mybir.dt.float32, mybir.dt.float32r, mybir.dt.float16, mybir.dt.bfloat16
    ALU, ACT, AX = mybir.AluOpType, mybir.ActivationFunctionType, mybir.AxisListType.X
    q_dram = nc.dram_tensor("q_scratch", [ROWS, HALVES * GH, T], f32, kind="Internal").ap()
    x_t = x.rearrange("(b p) d -> p b d", p=P)
    out_t = out.rearrange("(b p) d -> p b d", p=P)
    ctx_t = ctxT.rearrange("(k p) t -> p k t", p=P)

    def weight_view(w):
        return w.rearrange("(k p) n -> p k n", p=P)

    with ExitStack() as ctx:
        def sb(name, shape, dt, where=ctx):
            return where.enter_context(nc.sbuf_tensor(name, shape, dt))

        def sem(name):
            return ctx.enter_context(nc.semaphore(name))

        ident = sb("ident", [P, P], f32)
        xres = sb("xres", [P, NB, D], f32)
        stats = sb("stats", [P, NB, 6], f32)
        mv = sb("mv", [P, NB, 2], f32)
        rstd = sb("rstd", [P, NB], f32)
        var = sb("var", [P, NB], f32)
        root = sb("root", [P, NB], f32)
        newton = sb("newton", [P, NB], f32)
        wr_raw = sb("wr_raw", [P, KC, E], f32)
        wr_hi = sb("wr_hi", [P, KC, E], f32r)
        wr_lo = sb("wr_lo", [P, KC, E], f32r)
        raw = [sb(f"raw{i}", [P, WU], f32) for i in range(2)]
        Wu = [sb(f"W{u}", [P, 2, WU], f32r) for u in range(EARLY)]
        att = ExitStack()
        with att:
            wq = sb("wq", [P, KC, D], f32, att)
            wk = sb("wk", [P, KC, HALVES * ROWS], f32, att)
            wv = sb("wv", [P, KC, GROUPS * HD], f32, att)
            wfc = sb("wfc", [P, KC, D], f32, att)
            bias = sb("bias", [P, D], f32, att)
            cT = sb("cT", [P, KC, T], f32, att)
            xn = sb("xn", [P, CT, D], f32, att)
            xT = sb("xT", [P, KC, CH], f32, att)
            qhl = [sb(f"qhl{c}", [P, HALVES, 2, CH], f32r, att) for c in range(QR)]
            kst = sb("kst", [P, HALVES, T], f32r, att)
            minus_hi = sb("minus_hi", [P, 1], f32, att)
            in_part = sb("in_part", [P, PARTS, QUADS], f32, att)
            own = sb("own", [P, QUADS], f32, att)
            vres = sb("vres", [P, CT, GROUPS, HD], f32, att)
            V3 = sb("V3", [P, NB, GROUPS, VW], bf16, att)
            qs = [sb(f"qs{i}", [P, QCOLS], f32r, att) for i in range(STACKS)]
            ks = [sb(f"ks{i}", [P, QUADS, HALVES, S], f32r, att) for i in range(STACKS)]
            p32 = [sb(f"p32_{i}", [P, 2 * GH * S], f32, att) for i in range(PR)]
            phi = [sb(f"phi_{i}", [P, 2 * GH * S], f16, att) for i in range(PR)]
            plo = [sb(f"plo_{i}", [P, 2 * GH * S], f16, att) for i in range(PR)]
            mx = [sb(f"mx{i}", [P, QUADS, HALVES, GH], f32, att) for i in range(STACKS)]
            mrow = [sb(f"mrow{i}", [HEADS, P], f32r, att) for i in range(STACKS)]
            rden = sb("rden", [P, HEADS // 2], f32, att)
            osum = sb("osum", [P, HEADS // 2, HD], f32, att)
            O = sb("O", [P, D], f32, att)
            OT = sb("OT", [P, KC, P], f32, att)
        ex = ExitStack()
        with ex:
            Wu += [sb(f"W{u}", [P, 2, WU], f32r, ex) for u in range(EARLY, UNITS - LATE)]
            x2hi = sb("x2hi", [P, KC, T], f32r, ex)
            x2lo = sb("x2lo", [P, KC, T], f32r, ex)
            cwT = sb("cwT", [2 * E, T], f32r, ex)
            sel = sb("sel", [2 * E, E, P], f32r, ex)
            h = [sb(f"h{i}", [P, CH], f32, ex) for i in range(2)]
            ghi = [sb(f"ghi{i}", [P, CH], f32r, ex) for i in range(GR)]
            glo = [sb(f"glo{i}", [P, CH], f32r, ex) for i in range(GR)]
            router = ExitStack()
            with router:
                xn2 = sb("xn2", [P, CT, D], f32, router)
                lg = sb("lg", [P, NB, E], f32, router)
                pr = sb("pr", [P, NB, E], f32, router)
                above = sb("above", [P, NB, E], f32, router)
                tie = sb("tie", [P, NB, E], f32, router)
                rank = [sb("rank", [P, NB, E], f32, router), lg]
                top8 = sb("top8", [P, NB, 8], f32, router)
                cw = sb("cw", [P, NB, 2, E], f32, router)
                one = sb("one", [P, NB, 1], f32, router)
            Wu += [sb(f"W{u}", [P, 2, WU], f32r, ex) for u in range(UNITS - LATE, UNITS)]

        ysb = [raw[m][:, 0:CH] for m in range(KC)]

        def banks(shapes):
            with ExitStack() as here:
                return [here.enter_context(nc.psum_tensor(name, shape, f32)) for name, shape in shapes]

        psT, psK, psV, *psQ = banks([("psT", [P, KC, CH]), ("psK", [ROWS, CH]), ("psV", [P, 2 * CT, GROUPS * HD]),
                                     ("psQ0", [P, CH]), ("psQ1", [P, CH])])
        psST0, psST1, psO, psM, psS0, psS1 = banks([
            ("psST0", [P, 2 * GH * S]), ("psST1", [P, 2 * GH * S]), ("psO", [P, HEADS // 2, VW]), ("psM", [P, 2 * D]),
            ("psS0", [P, GH * S]), ("psS1", [P, GH * S])])
        psS, psST = [psS0, psS1], [psST0, psST1]
        psH0, psH1, psG0, psG1, psC0, psC1, psY0, psY1 = banks([
            (name, [P, CH]) for name in ("psH0", "psH1", "psG0", "psG1", "psC0", "psC1", "psY0", "psY1")])
        psH, psG, psC, psY = [psH0, psH1], [psG0, psG1], [psC0, psC1], [psY0, psY1]
        cwT_banks = [psC1, psY0, psY1, psC0]

        x_in = [sem(f"x_in{c}") for c in range(NC)]
        ctx_in = [sem(f"ctx_in{c}") for c in range(NC)]
        wq_in, wk_in, wv_in, wfc_in, bias_in, wr_in = (sem(n) for n in (
            "wq_in", "wk_in", "wv_in", "wfc_in", "bias_in", "wr_in"))
        raw_in = [sem(f"raw_in{i}") for i in range(2)]
        ident_zero, ident_made, fill_made = sem("ident_zero"), sem("ident_made"), sem("fill_made")
        ks_zero, ks_ready, ks_made = sem("ks_zero"), sem("ks_ready"), sem("ks_made")
        part_ones, part_made = sem("part_ones"), sem("part_made")
        dve_steps = sem("dve_steps")
        var_made, root_made = sem("var_made"), sem("root_made")
        xn_made, xT_psum, xT_made = sem("xn_made"), sem("xT_psum"), sem("xT_made")
        k_psum, v_psum, q_psum = sem("k_psum"), sem("v_psum"), sem("q_psum")
        k_hi_made, k_lo_made, v_made = sem("k_hi_made"), sem("k_lo_made"), sem("v_made")
        q_hi_made, q_lo_made = sem("q_hi_made"), sem("q_lo_made")
        stacked = [sem(f"stacked{c}") for c in range(NC)]
        stack_in = [sem(f"stack_in{i}") for i in range(STACKS)]
        bias_added = sem("bias_added")
        s_psum, max_made, maxT_psum, row_made = sem("s_psum"), sem("max_made"), sem("maxT_psum"), sem("row_made")
        row_in = [sem(f"row_in{i}") for i in range(STACKS)]
        st_psum, phi_made, p32_made, plo_made = sem("st_psum"), sem("phi_made"), sem("p32_made"), sem("plo_made")
        pv_done, o_read, half_made = sem("pv_done"), sem("o_read"), sem("half_made")
        oT_psum, oT_made, fc_done, x1_made = sem("oT_psum"), sem("oT_made"), sem("fc_done"), sem("x1_made")
        w_hi, w_lo, wr_cut = sem("w_hi"), sem("w_lo"), sem("wr_cut")
        x2_psum, x2_hi_made, x2_lo_made = sem("x2_psum"), sem("x2_hi_made"), sem("x2_lo_made")
        logits, shifted, exps, cw_made = sem("logits"), sem("shifted"), sem("exps"), sem("cw_made")
        cwT_psum, cwT_made, sel_zero, sel_made = sem("cwT_psum"), sem("cwT_made"), sem("sel_zero"), sem("sel_made")
        up_done, gate_done, silu_done, prod_done = sem("up_done"), sem("gate_done"), sem("silu_done"), sem("prod_done")
        ghi_made, glo_made, down_done = sem("ghi_made"), sem("glo_made"), sem("down_done")
        y_made, yT_psum, final, stored = sem("y_made"), sem("yT_psum"), sem("final"), sem("stored")

        class Steps:

            def __init__(self, eng, s):
                self.eng, self.s, self.n = eng, s, 0

            def link(self, ins):
                ins.then_inc(self.s, 1)
                self.n = self.n + 1
                self.eng.wait_ge(self.s, self.n)

        def known(v):
            return isinstance(v, int)

        def wait(eng, s, v):
            if not known(v) or v > 0:
                eng.wait_ge(s, v)

        def batches(eng, body):
            body(0, 0, 0)
            with eng.Fori(0, (NB - STACKS) // STACKS) as i:
                for u in range(1, STACKS + 1):
                    body(STACKS * i + u, u % STACKS, i + u // STACKS)
            for b in range(NB - STACKS + 1, NB):
                body(b, b % STACKS, b // STACKS)

        CUTS = ((0,), (1, 2), (3, 4), (5,))
        FIRST = (slice(0, CT), slice(CT, NB))
        Q_PART, K_PART = (0, 1, 0), (0, 0, 1)

        def first(b):
            return known(b) and b == 0

        def last(b):
            return known(b) and b == NB - 1

        def slot_after(slot, turn, by):
            return (slot + by) % STACKS, turn + (slot + by) // STACKS

        def exists(b):
            return not known(b) or 0 <= b < NB

        STACKED = 16 * PARTS * HALVES

        def g_slot_used(n, u):
            return n - (GR - 1) if u >= GR else n - (UNITS % GR) + 1 if u < UNITS % GR else n - (UNITS % GR) - GR + 1

        block = ctx.enter_context(nc.Block())

        @block.sync
        def _(sp):
            for c in range(NC):
                sp.dma_start(xres[:, c * CT:(c + 1) * CT, :], x_t[:, c * CT:(c + 1) * CT, :]).then_inc(x_in[c], 16)

            def load_stack(b, slot):
                sp.dma_start(qs[slot][0:ROWS, :].bitcast(f32).rearrange("p (g t) -> p g t", t=S),
                             q_dram.rearrange("p g (b t) -> p g b t", t=S)[:, :, bass.ds(b, 1), :]
                             .rearrange("p g b t -> p g (b t)")).then_inc(stack_in[slot], 16)

            def store(c, part):
                for half in range(HALVES):
                    sp.dma_start(q_dram[part * GROUP_ROWS:(part + 1) * GROUP_ROWS, half * GH:(half + 1) * GH,
                                        c * CH:(c + 1) * CH].rearrange("r j t -> j r t"),
                                 qhl[c % QR][:, half, Q_PART[part], :].bitcast(f32)).then_inc(stacked[c], 16)

            for c in range(NC):
                sp.wait_ge(q_hi_made, HALVES * (c + 1))
                for part in (0, 2):
                    store(c, part)
                sp.wait_ge(q_lo_made, HALVES * (c + 1))
                store(c, 1)
                if c == 0:
                    sp.wait_ge(stacked[0], STACKED)
                    for b in range(STACKS):
                        load_stack(b, b)
            sp.wait_ge(fill_made, 1)

            def sp_batch(b, slot, turn):
                sp.wait_ge(row_made, b + 1)
                sp.dma_start(qs[slot][ROWS:ROWS + QUADS, :].bitcast(f32), mrow[slot][:].bitcast(f32))\
                  .then_inc(row_in[slot], 16)
                if first(b):
                    for c in range(1, NC):
                        sp.wait_ge(stacked[c], STACKED)
                elif exists(b + STACKS - 1):
                    sp.wait_ge(st_psum, PAIRS * b)
                    load_stack(b + STACKS - 1, (slot + STACKS - 1) % STACKS)

            batches(sp, sp_batch)
            for c in range(NC):
                sp.wait_ge(final, 2 * (c + 1))
                sp.dma_start(out_t[:, c * CT:(c + 1) * CT, :], xres[:, c * CT:(c + 1) * CT, :]).then_inc(stored, 16)
            sp.wait_ge(stored, 16 * NC)

        @block.scalar
        def _(act):
            act.dma_start(wk[:], weight_view(WkT)).then_inc(wk_in, 16)
            act.dma_start(cT[:, :, 0:CH], ctx_t[:, :, 0:CH]).then_inc(ctx_in[0], 16)
            act.dma_start(wv[:], weight_view(WvT)).then_inc(wv_in, 16)
            act.dma_start(wq[:], weight_view(WqT)).then_inc(wq_in, 16)
            for c in range(1, NC):
                act.dma_start(cT[:, :, c * CH:(c + 1) * CH], ctx_t[:, :, c * CH:(c + 1) * CH]).then_inc(ctx_in[c], 16)
            act.dma_start(bias[:], bfc.partition_broadcast(P)).then_inc(bias_in, 16)
            act.dma_start(wfc[:], weight_view(WfcT)).then_inc(wfc_in, 16)
            act.dma_start(wr_raw[:], weight_view(wr)).then_inc(wr_in, 16)

            for n, bs in enumerate(FIRST):
                act.wait_ge(var_made, n + 1)
                act.activation(root[:, bs], var[:, bs], ACT.Sqrt).then_inc(root_made, 1)
            for c in range(NC):
                for half in range(HALVES):
                    act.wait_ge(k_psum, HALVES * c + half + 1)
                    act.activation(kst[0:ROWS, half, c * CH:(c + 1) * CH], psK[:], ACT.Copy).then_inc(k_hi_made, 1)
                act.wait_ge(xT_psum, c + 1)
                wait(act, q_psum, 2 * c)
                act.activation(xT[:], psT[:], ACT.Copy).then_inc(xT_made, 1)
                for half in range(HALVES):
                    act.wait_ge(q_psum, 2 * c + half + 1)
                    if half == 0 and c >= QR:
                        act.wait_ge(stacked[c - QR], STACKED)
                    act.activation(qhl[c % QR][:, half, 0, :], psQ[half][:], ACT.Copy).then_inc(q_hi_made, 1)

            def act_oT(b):
                act.wait_ge(oT_psum, b + 1)
                act.activation(OT[:].rearrange("p k t -> p (k t)"), psM[:, 0:D], ACT.Copy).then_inc(oT_made, 1)

            def act_batch(b, slot, turn):
                for p in range(PAIRS):
                    n, r = PAIRS * b + p, p
                    if p == 3 and not first(b):
                        act_oT(b - 1)
                    act.wait_ge(st_psum, n + 1)
                    wait(act, pv_done, n - PR + 1)
                    act.activation(phi[r][:], psST[p % 2][:], ACT.Exp, scale=SCALE).then_inc(phi_made, 1)
                    wait(act, plo_made, n - PR + 1)
                    act.activation(p32[r][:], psST[p % 2][:], ACT.Exp, scale=SCALE).then_inc(p32_made, 1)

            batches(act, act_batch)
            act_oT(NB - 1)

            act.wait_ge(var_made, len(FIRST) + 1)
            act.activation(root[:], var[:], ACT.Sqrt).then_inc(root_made, 1)
            for c in range(NC):
                act.wait_ge(x2_psum, c + 1)
                for k in range(KC):
                    act.activation(x2hi[:, k, c * CH:(c + 1) * CH], (psH, psG)[c % 2][k][:], ACT.Copy)\
                       .then_inc(x2_hi_made, 1)
            act.wait_ge(shifted, 1)
            act.activation(pr[:], lg[:], ACT.Exp).then_inc(exps, 1)
            for c in range(NC):
                act.wait_ge(cwT_psum, c + 1)
                act.activation(cwT[:, c * CH:(c + 1) * CH], cwT_banks[c][0:2 * E, :], ACT.Copy).then_inc(cwT_made, 1)

            def act_y(c):
                act.wait_ge(down_done, UNITS * (c + 1))
                for m in range(KC):
                    act.activation(ysb[m], psY[m][:], ACT.Copy).then_inc(y_made, 1)

            def act_chunk(c):
                for u in range(UNITS):
                    n = UNITS * c + u
                    act.wait_ge(up_done, n + 1)
                    wait(act, glo_made, n - 1)
                    act.activation(h[u % 2][:], psH[u % 2][:], ACT.Silu).then_inc(silu_done, 1)
                    act.wait_ge(prod_done, n + 1)
                    wait(act, down_done, g_slot_used(n, u))
                    act.activation(ghi[u % GR][:], h[u % 2][:], ACT.Copy).then_inc(ghi_made, 1)
                    if u == 1 and not first(c):
                        act_y(c - 1)

            act_chunk(0)
            with act.Fori(1, NC) as c:
                act_chunk(c)
            act_y(NC - 1)

        @block.gpsimd
        def _(pool):
            pool.memset(ident[:], 0.0).then_inc(ident_zero, 1)
            pool.wait_ge(ident_zero, 1)
            pool.affine_select(out=ident[:], in_=ident[:], compare_op=ALU.not_equal, fill=1.0, base=0,
                               pattern=[[-1, P]], channel_multiplier=1).then_inc(ident_made, 1)

            def load_raw(u):
                wait(pool, w_lo, u - 1)
                pool.dma_start(raw[u % 2][:], W[u]).then_inc(raw_in[u % 2], 16)

            def cut_lo(u):
                pool.wait_ge(w_hi, u + 1)
                pool.tensor_tensor(Wu[u][:, 1, :], raw[u % 2][:], Wu[u][:, 0, :].bitcast(f32), ALU.subtract)\
                    .then_inc(w_lo, 1)
                if u + 2 < UNITS:
                    load_raw(u + 2)

            load_raw(0)
            load_raw(1)
            pool.memset(in_part[:], 1.0).then_inc(part_ones, 1)
            pool.wait_ge(part_ones, 1)
            pool.affine_select(out=in_part[:], in_=in_part[:], compare_op=ALU.is_ge, fill=0.0, base=0,
                               pattern=[[-GROUP_ROWS, PARTS], [-HD, QUADS]], channel_multiplier=1).then_inc(part_ones, 1)
            pool.wait_ge(part_ones, 2)
            pool.affine_select(out=in_part[:], in_=in_part[:], compare_op=ALU.is_ge, fill=0.0, base=HD - 1,
                               pattern=[[GROUP_ROWS, PARTS], [HD, QUADS]], channel_multiplier=-1).then_inc(part_made, 1)
            pool.wait_ge(ks_zero, 1)
            pool.wait_ge(part_made, 1)
            for slot in range(STACKS):
                if slot > 0:
                    pool.wait_ge(ks_ready, slot)
                rows = ks[slot][ROWS:P, :, :, :].rearrange("p q h t -> p q (h t)")
                pool.affine_select(out=rows, in_=rows.bitcast(f32), compare_op=ALU.not_equal, fill=-1.0, base=0,
                                   pattern=[[-1, QUADS], [0, HALVES * S]], channel_multiplier=1).then_inc(ks_ready, 1)
            pool.wait_ge(ks_ready, STACKS)
            for u in range(EARLY):
                cut_lo(u)
            pool.wait_ge(bias_in, 16)
            for c in range(NC):
                pool.wait_ge(xn_made, CT * (c + 1))
                here = xres[:, c * CT:(c + 1) * CT, :]
                pool.tensor_tensor(here, here, bias[:].unsqueeze(1).broadcast_to([P, CT, D]), ALU.add)\
                    .then_inc(bias_added, 1)

            def pool_batch(b, slot, turn):
                for p in range(PAIRS):
                    n, r = PAIRS * b + p, p
                    pool.wait_ge(p32_made, n + 1)
                    wait(pool, pv_done, n - PR + 1)
                    pool.tensor_tensor(plo[r][:], p32[r][:], phi[r][:], ALU.subtract).then_inc(plo_made, 1)

            batches(pool, pool_batch)

            pool.wait_ge(x1_made, NB)
            pool.memset(sel[:].bitcast(f32), 0.0).then_inc(sel_zero, 1)
            for part in range(2):
                pool.wait_ge(sel_zero, part + 1)
                pool.affine_select(out=sel[:], in_=sel[:].bitcast(f32), compare_op=ALU.not_equal, fill=1.0,
                                   base=-E * part, pattern=[[-1, E], [0, P]], channel_multiplier=1)\
                    .then_inc(sel_zero if part == 0 else sel_made, 1)
            for u in range(EARLY, UNITS):
                cut_lo(u)

        @block.vector
        def _(dve):
            steps = Steps(dve, dve_steps)

            def make_rstd(times, bs):
                steps.link(dve.tensor_scalar(var[:, bs], mv[:, bs, 1], EPS, None, ALU.add))
                dve.tensor_copy(newton[:, bs], var[:, bs]).then_inc(var_made, 1)
                dve.wait_ge(root_made, times)
                steps.link(dve.reciprocal(rstd[:, bs], root[:, bs]))
                steps.link(dve.tensor_tensor(newton[:, bs], rstd[:, bs], rstd[:, bs], ALU.mult))
                steps.link(dve.tensor_tensor(newton[:, bs], newton[:, bs], var[:, bs], ALU.mult))
                steps.link(dve.tensor_scalar(newton[:, bs], newton[:, bs], -0.5, 1.5, ALU.mult, ALU.add))
                steps.link(dve.tensor_tensor(rstd[:, bs], rstd[:, bs], newton[:, bs], ALU.mult))

            def cut_hi(u):
                dve.wait_ge(raw_in[u % 2], 16 * (u // 2 + 1))
                dve.tensor_copy(Wu[u][:, 0, :], raw[u % 2][:]).then_inc(w_hi, 1)

            def normed(to, b):
                return dve.tensor_scalar(to, xres[:, b, :], mv[:, b, 0:1], rstd[:, b:b + 1], ALU.subtract, ALU.mult)

            def maximum(b, g, slot):
                dve.wait_ge(s_psum, GROUPS * b + g + 1)
                if g == 0:
                    wait(dve, maxT_psum, b - STACKS + 2)
                dve.tensor_reduce(mx[slot][:, :, g // GH, g % GH], psS[g % 2][:].rearrange("p (q t) -> p q t", q=QUADS),
                                  AX, ALU.max).then_inc(max_made, 1)

            def max_row(b, slot):
                dve.wait_ge(maxT_psum, b + 1)
                dve.tensor_copy(mrow[slot][:], psM[0:HEADS, 0:P]).then_inc(row_made, 1)

            def first_maxima(i):
                for g in (2 * i, 2 * i + 1):
                    maximum(0, g, 0)

            for slot in range(STACKS):
                ins = dve.memset(ks[slot][ROWS:P, :, :, :].bitcast(f32), 0.0)
            ins.then_inc(ks_zero, 1)
            steps.link(dve.memset(minus_hi[:], 0.0))
            dve.memset(minus_hi[2 * GROUP_ROWS:ROWS, :], -1.0)
            for n, bs in enumerate(FIRST):
                for b in range(bs.start, bs.stop):
                    if b % CT == 0:
                        dve.wait_ge(x_in[b // CT], 16)
                    ins = dve.bn_stats(stats[:, b, :], xres[:, b, :])
                steps.link(ins)
                for b in range(bs.start, bs.stop):
                    ins = dve.bn_aggr(mv[:, b, :], stats[:, b, :])
                steps.link(ins)
                make_rstd(n + 1, bs)
                if n == 0:
                    for t in range(CT):
                        normed(xn[:, t, :], t).then_inc(xn_made, 1)
            dve.wait_ge(part_made, 1)
            dve.tensor_reduce(own[:], in_part[:].rearrange("p s q -> p q s"), AX, ALU.add)
            for slot in range(STACKS):
                dve.memset(qs[slot][ROWS:P, :].bitcast(f32), 0.0)
            steps.link(dve.memset(V3[:], 1.0))
            dve.memset(newton[:], 0.0).then_inc(fill_made, 1)

            def keys_lo(c, half):
                here = kst[0:ROWS, half, c * CH:(c + 1) * CH]
                dve.wait_ge(k_hi_made, HALVES * c + half + 1)
                dve.scalar_tensor_tensor(here, here.bitcast(f32), minus_hi[0:ROWS, :], psK[:], ALU.mult, ALU.add)\
                   .then_inc(k_lo_made, 1)

            def block_keys(b, slot):
                for quad in range(QUADS):
                    ins = dve.tensor_scalar(ks[slot][0:ROWS, quad, :, :],
                                            kst[0:ROWS, :, bass.ds(b * S, S)].bitcast(f32),
                                            own[0:ROWS, quad:quad + 1], None, ALU.mult)
                ins.then_inc(ks_made, 1)

            for c in range(NC):
                if c > 0:
                    dve.wait_ge(xT_psum, c)
                    for t in range(CT):
                        normed(xn[:, t, :], c * CT + t).then_inc(xn_made, 1)
                if c == NC - 1:
                    first_maxima(0)
                keys_lo(c, 0)
                dve.wait_ge(v_psum, c + 1)
                vps = psV[:, 0:CT, :].rearrange("p t (g d) -> p t g d", g=GROUPS)
                part = [V3[:, c * CT:(c + 1) * CT, :, HD * i:HD * (i + 1)] for i in range(3)]
                steps.link(dve.tensor_copy(part[0], vps))
                steps.link(dve.tensor_tensor(vres[:], vps, part[0], ALU.subtract))
                steps.link(dve.tensor_copy(part[1], vres[:]))
                steps.link(dve.tensor_tensor(vres[:], vres[:], part[1], ALU.subtract))
                dve.tensor_copy(part[2], vres[:]).then_inc(v_made, 1)
                if c == NC - 1:
                    first_maxima(1)
                keys_lo(c, 1)
                if c == NC - 1:
                    first_maxima(2)
                for half in range(HALVES):
                    dve.wait_ge(q_hi_made, HALVES * c + half + 1)
                    if half == 0 and c >= QR:
                        dve.wait_ge(stacked[c - QR], STACKED)
                    dve.tensor_tensor(qhl[c % QR][:, half, 1, :], psQ[half][:], qhl[c % QR][:, half, 0, :].bitcast(f32),
                                      ALU.subtract).then_inc(q_lo_made, 1)
                if c == 0:
                    dve.wait_ge(k_lo_made, HALVES)
                    dve.wait_ge(ks_ready, STACKS)
                    for b in range(STACKS):
                        block_keys(b, b)
                for u in CUTS[c]:
                    cut_hi(u)

            def combine(b, half):
                dve.wait_ge(pv_done, PAIRS * b + 2 * half + 2)
                wait(dve, half_made, 2 * b + half)
                dve.reciprocal(rden[:], psO[:, :, 3 * HD])
                dve.tensor_reduce(osum[:], psO[:, :, 0:3 * HD].rearrange("p h (s d) -> p h d s", s=3), AX, ALU.add)\
                   .then_inc(o_read, 1)
                dve.wait_ge(o_read, 2 * b + half + 1)
                if half == 0:
                    wait(dve, oT_psum, b)
                dve.tensor_tensor(O[:, half * P:(half + 1) * P].rearrange("p (h d) -> p h d", d=HD), osum[:],
                                  rden[:].unsqueeze(2).broadcast_to([P, HEADS // 2, HD]), ALU.mult)\
                   .then_inc(half_made, 1)

            def residual(b):
                dve.wait_ge(fc_done, b + 1)
                here = xres[:, bass.ds(b, 1), :].rearrange("p b d -> p (b d)")
                dve.tensor_tensor(here, psM[:, D:2 * D], here, ALU.add).then_inc(x1_made, 1)
                dve.wait_ge(x1_made, b + 1)
                dve.bn_stats(stats[:, bass.ds(b, 1), :].rearrange("p b s -> p (b s)"), here)

            def dve_batch(b, slot, turn):
                one_on, two_on, three_on = ((slot + i) % STACKS for i in (1, 2, 3))
                if exists(b + 1):
                    for g in (4, 5):
                        maximum(b + 1, g, one_on)
                if not first(b) and exists(b + 3):
                    dve.wait_ge(st_psum, PAIRS * b)
                    block_keys(b + 3, three_on)
                if exists(b + 1):
                    for g in (6, 7):
                        maximum(b + 1, g, one_on)
                if not first(b):
                    combine(b - 1, 1)
                if exists(b + 1):
                    max_row(b + 1, one_on)
                if exists(b + 2):
                    for g in range(4):
                        maximum(b + 2, g, two_on)
                if not first(b):
                    residual(b - 1)
                combine(b, 0)

            first_maxima(3)
            max_row(0, 0)
            for g in range(4):
                maximum(1, g, 1)
            dve.wait_ge(bias_added, NC)
            batches(dve, dve_batch)
            combine(NB - 1, 1)
            residual(NB - 1)
            steps.link(dve.tensor_copy(newton[:], rstd[:]))
            for b in range(NB):
                ins = dve.bn_aggr(mv[:, b, :], stats[:, b, :])
            steps.link(ins)
            make_rstd(len(FIRST) + 1, slice(0, NB))
            for c in range(NC):
                for t in range(CT):
                    if t == 0:
                        wait(dve, x2_psum, c)
                    normed(xn2[:, t, :], c * CT + t).then_inc(xn_made, 1)
                if c == 0:
                    dve.wait_ge(wr_in, 16)
                    steps.link(dve.tensor_copy(wr_hi[:], wr_raw[:]))
                    dve.tensor_tensor(wr_lo[:], wr_raw[:], wr_hi[:].bitcast(f32), ALU.subtract).then_inc(wr_cut, 1)
                for k in range(KC):
                    dve.wait_ge(x2_hi_made, KC * c + k + 1)
                    here = slice(c * CH, (c + 1) * CH)
                    dve.tensor_tensor(x2lo[:, k, here], (psH, psG)[c % 2][k][:], x2hi[:, k, here].bitcast(f32),
                                      ALU.subtract).then_inc(x2_lo_made, 1)
            dve.wait_ge(logits, 1)
            lps = psC[0][:, 0:NB * E].rearrange("p (b e) -> p b e", e=E)
            per_expert = [P, NB, E]
            steps.link(dve.tensor_reduce(one[:, :, 0], lps, AX, ALU.max))
            dve.tensor_tensor(lg[:], lps, one[:].broadcast_to(per_expert), ALU.subtract).then_inc(shifted, 1)
            dve.wait_ge(exps, 1)
            steps.link(dve.tensor_reduce(one[:, :, 0], pr[:], AX, ALU.add))
            steps.link(dve.reciprocal(one[:], one[:]))
            steps.link(dve.tensor_tensor(pr[:], pr[:], one[:].broadcast_to(per_expert), ALU.mult))
            for b in range(NB):
                ins = dve.max(top8[:, b, :], pr[:, b, :])
            steps.link(ins)
            fourth = top8[:, :, TOP - 1:TOP].broadcast_to(per_expert)
            dve.tensor_tensor(above[:], pr[:], fourth, ALU.is_gt)
            steps.link(dve.tensor_tensor(tie[:], pr[:], fourth, ALU.is_equal))
            steps.link(dve.tensor_reduce(one[:, :, 0], above[:], AX, ALU.add))
            src = tie
            for i in range(4):
                dst, step = rank[i % 2], 1 << i
                dve.tensor_copy(dst[:, :, 0:step], src[:, :, 0:step])
                steps.link(dve.tensor_tensor(dst[:, :, step:], src[:, :, step:], src[:, :, 0:E - step], ALU.add))
                src = dst
            steps.link(dve.tensor_tensor(rank[0][:], src[:], one[:].broadcast_to(per_expert), ALU.add))
            steps.link(dve.scalar_tensor_tensor(rank[1][:], rank[0][:], float(TOP), tie[:], ALU.is_le, ALU.mult))
            steps.link(dve.tensor_tensor(rank[0][:], rank[1][:], above[:], ALU.add))
            steps.link(dve.tensor_tensor(lg[:], rank[0][:], pr[:], ALU.mult))
            steps.link(dve.tensor_reduce(one[:, :, 0], lg[:], AX, ALU.add))
            steps.link(dve.reciprocal(one[:], one[:]))
            steps.link(dve.tensor_scalar(one[:], one[:], TOP / (TOP + 1.0), None, ALU.mult))
            steps.link(dve.tensor_tensor(lg[:], lg[:], one[:].broadcast_to(per_expert), ALU.mult))
            steps.link(dve.tensor_copy(cw[:, :, 0, :].bitcast(f32r), lg[:]))
            dve.tensor_tensor(cw[:, :, 1, :].bitcast(f32r), lg[:], cw[:, :, 0, :], ALU.subtract).then_inc(cw_made, 1)

            def add_y(c):
                dve.wait_ge(yT_psum, c + 1)
                for i in range(2):
                    here = xres[:, bass.ds(c * CT + 2 * i, 2), :].rearrange("p b d -> p (b d)")
                    dve.tensor_tensor(here, psC[i][:], here, ALU.add).then_inc(final, 1)

            def dve_unit(n, u):
                hu, weights = h[u % 2][:], psC[u % 2][:]
                dve.wait_ge(silu_done, n + 1)
                dve.wait_ge(gate_done, n + 1)
                if u < SHARED:
                    dve.scalar_tensor_tensor(hu, hu, 1.0 / (TOP + 1), psG[u % 2][:], ALU.mult, ALU.mult)\
                       .then_inc(prod_done, 1)
                else:
                    steps.link(dve.tensor_tensor(hu, hu, psG[u % 2][:], ALU.mult))
                    dve.tensor_tensor(hu, hu, weights, ALU.mult).then_inc(prod_done, 1)
                dve.wait_ge(ghi_made, n + 1)
                wait(dve, down_done, g_slot_used(n, u))
                dve.tensor_tensor(glo[u % GR][:], hu, ghi[u % GR][:].bitcast(f32), ALU.subtract).then_inc(glo_made, 1)

            for u in range(UNITS):
                dve_unit(u, u)
                if EARLY + u < UNITS:
                    if EARLY + u >= UNITS - LATE:
                        dve.wait_ge(cwT_psum, NC)
                    cut_hi(EARLY + u)
            base = steps.n
            with dve.Fori(1, NC) as c:
                steps.n = base + E * (c - 1)
                for u in range(UNITS):
                    dve_unit(UNITS * c + u, u)
                    if u == 3:
                        add_y(c - 1)
            add_y(NC - 1)

        @block.tensor
        def _(pe):
            mm = pe.matmul

            def scores(b, g, slot, turn):
                if g == 0:
                    pe.wait_ge(stack_in[slot], 16 * (turn + 1))
                    pe.wait_ge(ks_made, b + 1)
                wait(pe, max_made, GROUPS * b + g - 1)
                mm(psS[g % 2][:], qs[slot][0:ROWS, g * S:(g + 1) * S], ks[slot][0:ROWS, :, g // GH, :],
                   start=True, stop=True).then_inc(s_psum, 1)

            def keys(c, half):
                wait(pe, k_lo_made, HALVES * c + half)
                for k in range(KC):
                    ins = mm(psK[:], wk[:, k, half * ROWS:(half + 1) * ROWS], cT[:, k, c * CH:(c + 1) * CH],
                             start=k == 0, stop=k == KC - 1)
                ins.then_inc(k_psum, 1)

            def first_scores(c, i):
                if c == NC - 1:
                    for g in (2 * i, 2 * i + 1):
                        scores(0, g, 0, 0)

            for c in range(NC):
                cs = c * CH
                if c == 0:
                    pe.wait_ge(wk_in, 16)
                pe.wait_ge(ctx_in[c], 16)
                keys(c, 0)
                first_scores(c, 0)
                if c == 0:
                    pe.wait_ge(wv_in, 16)
                wait(pe, v_made, c)
                for t in range(CT):
                    for k in range(KC):
                        ins = mm(psV[:, t, :], cT[:, k, cs + t * P:cs + (t + 1) * P], wv[:, k, :],
                                 start=k == 0, stop=k == KC - 1)
                ins.then_inc(v_psum, 1)
                keys(c, 1)
                first_scores(c, 1)
                if c == 0:
                    pe.wait_ge(ident_made, 1)
                wait(pe, xT_made, c)
                for t in range(CT):
                    pe.wait_ge(xn_made, c * CT + t + 1)
                    for k in range(KC):
                        ins = pe.transpose(psT[:, k, t * P:(t + 1) * P], xn[:, t, k * P:(k + 1) * P], ident[:])
                ins.then_inc(xT_psum, 1)
                first_scores(c, 2)
                if c == 0:
                    pe.wait_ge(wq_in, 16)
                pe.wait_ge(xT_made, c + 1)
                for half in range(HALVES):
                    wait(pe, q_lo_made, HALVES * (c - 1) + half + 1)
                    for k in range(KC):
                        ins = mm(psQ[half][:], wq[:, k, half * P:(half + 1) * P], xT[:, k, :],
                                 start=k == 0, stop=k == KC - 1)
                    ins.then_inc(q_psum, 1)

            def maxima_T(b, slot):
                pe.wait_ge(max_made, GROUPS * (b + 1))
                pe.transpose(psM[0:HEADS, 0:P], mx[slot][:].rearrange("p q h j -> p (q h j)"), ident[:]).then_inc(maxT_psum, 1)

            def scores_T(b, p, slot, turn):
                wait(pe, p32_made, PAIRS * b + p - 1)
                if p == 0:
                    pe.wait_ge(row_in[slot], 16 * (turn + 1))
                for i in range(2):
                    g = 2 * p + i
                    half = g // QUADS
                    ins = mm(psST[p % 2][:, i * GH * S:(i + 1) * GH * S], ks[slot][:, g % QUADS, half, :],
                             qs[slot][:, half * GH * S:(half + 1) * GH * S], start=True, stop=True)
                ins.then_inc(st_psum, 1)

            def values(b, p):
                r = p
                if p % 2 == 0:
                    wait(pe, o_read, 2 * b + p // 2)
                pe.wait_ge(phi_made, PAIRS * b + p + 1)
                pe.wait_ge(plo_made, PAIRS * b + p + 1)
                for i in range(2 * GH):
                    g = 2 * p + i // GH
                    v = V3[:, bass.ds(b, 1), g, 0:3 * HD + 1].rearrange("p b d -> p (b d)")
                    to = psO[:, (p % 2) * 2 * GH + i, 0:3 * HD + 1]
                    mm(to, phi[r][:, i * S:(i + 1) * S], v, start=True, stop=False)
                    ins = mm(to, plo[r][:, i * S:(i + 1) * S], v, start=False, stop=True)
                ins.then_inc(pv_done, 1)

            def transpose_O(b):
                pe.wait_ge(half_made, 2 * (b + 1))
                pe.wait_ge(row_made, min(b + 3, NB) if known(b) else b + 3)
                for k in range(KC):
                    ins = pe.transpose(psM[:, k * P:(k + 1) * P], O[:, k * P:(k + 1) * P], ident[:])
                ins.then_inc(oT_psum, 1)

            def project(b):
                pe.wait_ge(oT_made, b + 1)
                for k in range(KC):
                    ins = mm(psM[:, D:2 * D], OT[:, k, :], wfc[:, k, :], start=k == 0, stop=k == KC - 1)
                ins.then_inc(fc_done, 1)

            def pe_batch(b, slot, turn):
                one_on, two_on = slot_after(slot, turn, 1), slot_after(slot, turn, 2)
                for p in range(PAIRS):
                    if p == 3 and not first(b):
                        transpose_O(b - 1)
                    scores_T(b, p, slot, turn)
                    if p < 2:
                        if exists(b + 1):
                            scores(b + 1, 2 * p + 4, *one_on)
                            scores(b + 1, 2 * p + 5, *one_on)
                        if not first(b):
                            values(b - 1, p + 2)
                    else:
                        if exists(b + 2):
                            scores(b + 2, 2 * p - 4, *two_on)
                        if p == 2 and exists(b + 1):
                            maxima_T(b + 1, one_on[0])
                        if exists(b + 2):
                            scores(b + 2, 2 * p - 3, *two_on)
                        if p == 3 and not first(b):
                            project(b - 1)
                        values(b, p - 2)

            first_scores(NC - 1, 3)
            pe.wait_ge(xT_made, NC)
            pe.wait_ge(v_made, NC)
            pe.wait_ge(k_lo_made, HALVES * NC)
            pe.wait_ge(q_lo_made, HALVES * NC)
            maxima_T(0, 0)
            for g in range(4):
                scores(1, g, 1, 0)
            pe.wait_ge(wfc_in, 16)
            batches(pe, pe_batch)
            for p in (2, 3):
                values(NB - 1, p)
            transpose_O(NB - 1)
            project(NB - 1)

            for c in range(NC):
                wait(pe, x2_lo_made, KC * (c - 1))
                for t in range(CT):
                    pe.wait_ge(xn_made, NB + c * CT + t + 1)
                    for k in range(KC):
                        ins = pe.transpose((psH, psG)[c % 2][k][:, t * P:(t + 1) * P],
                                           xn2[:, t, k * P:(k + 1) * P], ident[:])
                ins.then_inc(x2_psum, 1)
            pe.wait_ge(wr_cut, 1)
            for c in range(NC):
                pe.wait_ge(x2_lo_made, KC * (c + 1))
                for b in range(c * CT, (c + 1) * CT):
                    to = psC[0][:, b * E:(b + 1) * E]
                    i = 0
                    for k in range(KC):
                        for xs, ws in ((x2hi, wr_hi), (x2hi, wr_lo), (x2lo, wr_hi)):
                            ins = mm(to, xs[:, k, b * P:(b + 1) * P], ws[:, k, :], start=i == 0, stop=i == 5)
                            i += 1
            ins.then_inc(logits, 1)

            def cut_products(to, w, col, c):
                i = 0
                for k in range(KC):
                    at = w[:, 0, col + k * P:col + (k + 1) * P], w[:, 1, col + k * P:col + (k + 1) * P]
                    for ws, xv in ((at[0], x2hi), (at[1], x2hi), (at[0], x2lo)):
                        ins = mm(to, ws, xv[:, k, bass.ds(c * CH, CH)], start=i == 0, stop=i == 3 * KC - 1)
                        i += 1
                return ins

            def up(c, u):
                n = UNITS * c + u
                pe.wait_ge(w_lo, u + 1)
                wait(pe, silu_done, n - 1)
                cut_products(psH[u % 2][:], Wu[u], 0, c).then_inc(up_done, 1)
                wait(pe, prod_done, n - 1)
                if SHARED <= u < SHARED + 2 and not first(c):
                    pe.wait_ge(final, 2 * c)
                ins = cut_products(psG[u % 2][:], Wu[u], D, c)
                if u >= SHARED:
                    ins = mm(psC[u % 2][:], sel[:, u - SHARED, :], cwT[:, bass.ds(c * CH, CH)], start=True, stop=True)
                ins.then_inc(gate_done, 1)

            def down(c, u):
                if u == 0:
                    wait(pe, y_made, KC * c)
                pe.wait_ge(glo_made, UNITS * c + u + 1)
                for m in range(KC):
                    at = 2 * D + m * P
                    i = 0
                    for wp, gs in ((0, ghi), (1, ghi), (0, glo)):
                        ins = mm(psY[m][:], Wu[u][:, wp, at:at + P], gs[u % GR][:], start=u == 0 and i == 0,
                                 stop=u == UNITS - 1 and i == 2)
                        i += 1
                ins.then_inc(down_done, 1)

            def transpose_y(c):
                pe.wait_ge(y_made, KC * (c + 1))
                pe.wait_ge(prod_done, UNITS * (c + 1))
                for t in range(CT):
                    for m in range(KC):
                        ins = pe.transpose(psC[t // 2][:, ((t % 2) * KC + m) * P:((t % 2) * KC + m + 1) * P],
                                           ysb[m][:, t * P:(t + 1) * P], ident[:])
                ins.then_inc(yT_psum, 1)

            def pe_chunk(c):
                for u in range(UNITS):
                    if u == SHARED and first(c):
                        pe.wait_ge(sel_made, 1)
                    if u == 2 and first(c):
                        weights_T()
                    up(c, u)
                    if u < 2:
                        if not first(c):
                            down(c - 1, UNITS - 2 + u)
                    else:
                        if u == 2 and not first(c):
                            transpose_y(c - 1)
                        down(c, u - 2)

            def weights_T():
                pe.wait_ge(cw_made, 1)
                for c in range(NC):
                    for t in range(CT):
                        ins = pe.transpose(cwT_banks[c][0:2 * E, t * P:(t + 1) * P],
                                           cw[:, c * CT + t, :, :].rearrange("p a e -> p (a e)"), ident[:])
                    ins.then_inc(cwT_psum, 1)
                pe.wait_ge(cwT_made, NC)

            pe_chunk(0)
            with pe.Fori(1, NC) as c:
                pe_chunk(c)
            down(NC - 1, UNITS - 2)
            down(NC - 1, UNITS - 1)
            transpose_y(NC - 1)


def kernel(x, ctx_2048, L0_xattn_Wq, L0_xattn_Wk, L0_xattn_Wv, L0_xattn_Wfc, L0_xattn_bfc, L0_ffn_w_router,
           L0_ffn_we1, L0_ffn_we3, L0_ffn_we2, L0_ffn_ws1, L0_ffn_ws3, L0_ffn_ws2):
    import numpy as np
    import concourse.bacc as bacc
    from concourse.bass_utils import run_bass_kernel_spmd

    def halves_of(w):
        return np.concatenate([w[..., k * P:(k + 1) * P, :] for k in range(KC)], axis=-1)

    def columns(w):
        return np.stack([w[:, u * P:(u + 1) * P] for u in range(SHARED)])

    a = {k: np.asarray(v) for k, v in dict(
        x=x, ctx=ctx_2048, Wq=L0_xattn_Wq, Wk=L0_xattn_Wk, Wv=L0_xattn_Wv, Wfc=L0_xattn_Wfc, bfc=L0_xattn_bfc,
        wr=L0_ffn_w_router, we1=L0_ffn_we1, we3=L0_ffn_we3, we2=L0_ffn_we2, ws1=L0_ffn_ws1, ws3=L0_ffn_ws3,
        ws2=L0_ffn_ws2).items()}
    wq = a["Wq"].reshape(HALVES, QUADS, GH, HD, D).transpose(0, 2, 1, 3, 4).reshape(D, D)
    shared = np.concatenate([halves_of(columns(a["ws1"])), halves_of(columns(a["ws3"])),
                             a["ws2"].reshape(SHARED, P, D)], axis=-1)
    experts = np.concatenate([halves_of(a["we1"]), halves_of(a["we3"]), a["we2"]], axis=-1)
    wk = np.repeat(a["Wk"].reshape(HALVES, 1, GROUP_ROWS, D), PARTS, axis=1).reshape(HALVES * ROWS, D)
    arrays = {
        "x": a["x"].reshape(T, D), "ctxT": a["ctx"].reshape(T, D).T, "WqT": wq.T, "WkT": wk.T, "WvT": a["Wv"].T,
        "WfcT": a["Wfc"].T, "bfc": a["bfc"], "wr": a["wr"], "W": np.concatenate([shared, experts]),
    }
    nc = bacc.Bacc("TRN2", target_bir_lowering=False, num_devices=1)
    args, given = {}, {}
    for name, v in arrays.items():
        v = np.ascontiguousarray(v)
        given[f"in_{name}"] = v
        args[name] = nc.dram_tensor(f"in_{name}", v.shape, mybir.dt.from_np(v.dtype), kind="ExternalInput").ap()
    out = nc.dram_tensor("out_0", (T, D), mybir.dt.float32, kind="ExternalOutput").ap()
    build(nc, out=out, **args)
    got = run_bass_kernel_spmd(nc, [given], core_ids=[0])
    return got.results[0]["out_0"].reshape(NB, S, D)
```

```python
import concourse.bass as bass
from concourse import mybir
from contextlib import ExitStack

P = 128
D = 256
KC = D // P
NB = 16
S = 128
T = NB * S
HD = 8
GROUPS, GH = 8, 4
HEADS = GROUPS * GH
QUADS = 4
HALVES = GROUPS // QUADS
PARTS = 3
GROUP_ROWS = QUADS * HD
ROWS = PARTS * GROUP_ROWS
SCALE = 1.0 / HD ** 0.5
EPS = 1e-5
CH = 512
NC = T // CH
CT = CH // P
E = 16
TOP = 4
SHARED = 4
UNITS = SHARED + E
WU = 3 * D
EARLY = 6
QCOLS = HALVES * GH * S
STACKS = 4
PAIRS = GROUPS // 2
PR = PAIRS
QR = 2
VW = 32
GR = 3
SR = 4
LATE = 2


def build(nc, x, ctxT, WqT, WkT, WvT, WfcT, bfc, wr, W, out):
    f32, f32r, f16, bf16 = mybir.dt.float32, mybir.dt.float32r, mybir.dt.float16, mybir.dt.bfloat16
    ALU, ACT, AX = mybir.AluOpType, mybir.ActivationFunctionType, mybir.AxisListType.X
    q_dram = nc.dram_tensor("q_scratch", [ROWS, HALVES * GH, T], f32, kind="Internal").ap()
    cw_dram = nc.dram_tensor("share_scratch", [E, T], f32, kind="Internal").ap()
    x_t = x.rearrange("(b p) d -> p b d", p=P)
    out_t = out.rearrange("(b p) d -> p b d", p=P)
    ctx_t = ctxT.rearrange("(k p) t -> p k t", p=P)

    def weight_view(w):
        return w.rearrange("(k p) n -> p k n", p=P)

    with ExitStack() as ctx:
        def sb(name, shape, dt, where=ctx):
            return where.enter_context(nc.sbuf_tensor(name, shape, dt))

        def sem(name):
            return ctx.enter_context(nc.semaphore(name))

        ident = sb("ident", [P, P], f32)
        xres = sb("xres", [P, NB, D], f32)
        stats = sb("stats", [P, NB, 6], f32)
        mv = sb("mv", [P, NB, 2], f32)
        rstd = sb("rstd", [P, NB], f32)
        var = sb("var", [P, NB], f32)
        root = sb("root", [P, NB], f32)
        warm = sb("warm", [P, 1], f32)
        shift = sb("shift", [P, NB], f32)
        newton = sb("newton", [P, NB], f32)
        wr_raw = sb("wr_raw", [P, KC, E], f32)
        wr_cut = sb("wr_cut", [P, KC, 2, E], f32r)
        raw = [sb(f"raw{i}", [P, WU], f32) for i in range(2)]
        Wu = [sb(f"W{u}", [P, 2, WU], f32r) for u in range(EARLY)]
        att = ExitStack()
        with att:
            cT = sb("cT", [P, KC, T], f32, att)
            qhl = [sb(f"qhl{c}", [P, HALVES, 2, CH], f32r, att) for c in range(QR)]
            xn = sb("xn", [P, CT, D], f32, att)
            xT = sb("xT", [P, KC, CH], f32, att)
            wq = sb("wq", [P, KC, D], f32, att)
            wk = sb("wk", [P, KC, HALVES * ROWS], f32, att)
            wv = sb("wv", [P, KC, GROUPS * HD], f32, att)
            wfc = sb("wfc", [P, KC, D], f32, att)
            bias = sb("bias", [P, D], f32, att)
            kst = sb("kst", [P, HALVES, T], f32r, att)
            minus_hi = sb("minus_hi", [P, 1], f32, att)
            in_part = sb("in_part", [P, PARTS, QUADS], f32, att)
            own = sb("own", [P, QUADS], f32, att)
            vres = sb("vres", [P, CT, GROUPS, HD], f32, att)
            V3 = sb("V3", [P, NB, GROUPS, VW], bf16, att)
            qs = [sb(f"qs{i}", [P, QCOLS], f32r, att) for i in range(STACKS)]
            ks = [sb(f"ks{i}", [P, QUADS, HALVES, S], f32r, att) for i in range(STACKS)]
            p32 = [sb(f"p32_{i}", [P, 2 * GH * S], f32, att) for i in range(PR)]
            phi = [sb(f"phi_{i}", [P, 2 * GH * S], f16, att) for i in range(PR)]
            plo = [sb(f"plo_{i}", [P, 2 * GH * S], f16, att) for i in range(PR)]
            mx = [sb(f"mx{i}", [P, QUADS, HALVES, GH], f32, att) for i in range(STACKS)]
            mrow = [sb(f"mrow{i}", [HEADS, P], f32r, att) for i in range(STACKS)]
            rden = sb("rden", [P, HEADS // 2], f32, att)
            osum = sb("osum", [P, HEADS // 2, HD], f32, att)
            O = sb("O", [P, D], f32, att)
            OT = sb("OT", [P, KC, P], f32, att)
        ex = ExitStack()
        with ex:
            x2hi = sb("x2hi", [P, KC, T], f32r, ex)
            x2lo = sb("x2lo", [P, KC, T], f32r, ex)
            shares = sb("shares", [P, SR, CH], f32, ex)
            Wu += [sb(f"W{u}", [P, 2, WU], f32r, ex) for u in range(EARLY, UNITS - LATE)]
            cwT = sb("cwT", [E, T], f32, ex)
            h = [sb(f"h{i}", [P, CH], f32, ex) for i in range(2)]
            ghi = [sb(f"ghi{i}", [P, CH], f32r, ex) for i in range(GR)]
            glo = [sb(f"glo{i}", [P, CH], f32r, ex) for i in range(GR)]
            router = ExitStack()
            with router:
                lg = sb("lg", [P, NB, E], f32, router)
                pr = sb("pr", [P, NB, E], f32, router)
                above = sb("above", [P, NB, E], f32, router)
                tie = sb("tie", [P, NB, E], f32, router)
                rank = [sb("rank", [P, NB, E], f32, router), lg]
                top8 = sb("top8", [P, NB, 8], f32, router)
                cw = sb("cw", [P, NB, E], f32, router)
                one = sb("one", [P, NB, 1], f32, router)
            Wu += [sb(f"W{u}", [P, 2, WU], f32r, ex) for u in range(UNITS - LATE, UNITS)]

        xn2 = [shares[:, 2 * i:2 * i + 2, :].rearrange("p a (t d) -> p (a t) d", d=D) for i in range(2)]
        logitsT = [shares[0:2 * E, c, :] for c in range(NC)]
        ysb = [raw[m][:, 0:CH] for m in range(KC)]

        def banks(shapes):
            with ExitStack() as here:
                return [here.enter_context(nc.psum_tensor(name, shape, f32)) for name, shape in shapes]

        psQ0, psQ1, psT, psK, psV = banks([("psQ0", [P, CH]), ("psQ1", [P, CH]), ("psT", [P, KC, CH]),
                                           ("psK", [ROWS, CH]), ("psV", [P, 2 * CT, GROUPS * HD])])
        psQ = [psQ0, psQ1]
        psST0, psST1, psO, psM, psS0, psS1 = banks([
            ("psST0", [P, 2 * GH * S]), ("psST1", [P, 2 * GH * S]), ("psO", [P, HEADS // 2, VW]), ("psM", [P, 2 * D]),
            ("psS0", [P, GH * S]), ("psS1", [P, GH * S])])
        psS, psST = [psS0, psS1], [psST0, psST1]
        psH0, psH1, psG0, psG1, psC0, psC1, psY0, psY1 = banks([
            (name, [P, CH]) for name in ("psH0", "psH1", "psG0", "psG1", "psC0", "psC1", "psY0", "psY1")])
        psH, psG, psC, psY = [psH0, psH1], [psG0, psG1], [psC0, psC1], [psY0, psY1]
        logitsT_banks = [psY0, psC0, psC1, psC0]
        x2_banks = [psY, psC]

        x_in = [sem(f"x_in{c}") for c in range(NC)]
        ctx_in = [sem(f"ctx_in{c}") for c in range(NC)]
        wq_in, wk_in, wv_in, wfc_in, bias_in, wr_in = (sem(n) for n in (
            "wq_in", "wk_in", "wv_in", "wfc_in", "bias_in", "wr_in"))
        raw_in = [sem(f"raw_in{i}") for i in range(2)]
        ident_zero, ident_made, fill_made = sem("ident_zero"), sem("ident_made"), sem("fill_made")
        ks_zero, ks_ready, ks_made = sem("ks_zero"), sem("ks_ready"), sem("ks_made")
        ks_other_made, own_made = sem("ks_other_made"), sem("own_made")
        part_ones, part_made = sem("part_ones"), sem("part_made")
        dve_steps = sem("dve_steps")
        warm_made, var_made, root_made = sem("warm_made"), sem("var_made"), sem("root_made")
        rstd_made = sem("rstd_made")
        xn_made, xT_psum, xT_made = sem("xn_made"), sem("xT_psum"), sem("xT_made")
        k_psum, v_psum, q_psum = sem("k_psum"), sem("v_psum"), sem("q_psum")
        k_hi_made, k_lo_made, v_made = sem("k_hi_made"), sem("k_lo_made"), sem("v_made")
        q_hi_made, q_lo_made = sem("q_hi_made"), sem("q_lo_made")
        stacked = [sem(f"stacked{c}") for c in range(NC)]
        stack_in = [sem(f"stack_in{i}") for i in range(STACKS)]
        bias_added = sem("bias_added")
        s_psum, max_made, maxT_psum, row_made = sem("s_psum"), sem("max_made"), sem("maxT_psum"), sem("row_made")
        row_in = [sem(f"row_in{i}") for i in range(STACKS)]
        st_psum, phi_made, p32_made, plo_made = sem("st_psum"), sem("phi_made"), sem("p32_made"), sem("plo_made")
        last_plo_made = sem("last_plo_made")
        pv_done, o_read, half_made = sem("pv_done"), sem("o_read"), sem("half_made")
        oT_psum, oT_made, fc_done, x1_made = sem("oT_psum"), sem("oT_made"), sem("fc_done"), sem("x1_made")
        w_hi, w_lo, wr_made = sem("w_hi"), sem("w_lo"), sem("wr_made")
        x2_psum, x2_hi_made, x2_lo_made = sem("x2_psum"), sem("x2_hi_made"), sem("x2_lo_made")
        logitsT_psum, logitsT_made = sem("logitsT_psum"), sem("logitsT_made")
        logits, shifted, exps, cw_made = sem("logits"), sem("shifted"), sem("exps"), sem("cw_made")
        cwT_psum, cwT_made = sem("cwT_psum"), sem("cwT_made")
        cw_stored = [sem(f"cw_stored{c}") for c in range(NC)]
        share_in = [sem(f"share_in{i}") for i in range(SR)]
        up_done, gate_done, silu_done, prod_done = sem("up_done"), sem("gate_done"), sem("silu_done"), sem("prod_done")
        ghi_made, glo_made, down_done = sem("ghi_made"), sem("glo_made"), sem("down_done")
        y_made, yT_psum, final, stored = sem("y_made"), sem("yT_psum"), sem("final"), sem("stored")

        class Steps:

            def __init__(self, eng, s):
                self.eng, self.s, self.n = eng, s, 0

            def link(self, ins):
                ins.then_inc(self.s, 1)
                self.n = self.n + 1
                self.eng.wait_ge(self.s, self.n)

        def known(v):
            return isinstance(v, int)

        def wait(eng, s, v):
            if not known(v) or v > 0:
                eng.wait_ge(s, v)

        def batches(eng, body, peeled=1):
            for b in range(peeled):
                body(b, b % STACKS, b // STACKS)
            with eng.Fori(0, (NB - STACKS) // STACKS) as i:
                for u in range(peeled, STACKS + peeled):
                    body(STACKS * i + u, u % STACKS, i + u // STACKS)
            for b in range(NB - STACKS + peeled, NB):
                body(b, b % STACKS, b // STACKS)

        CUTS = ((0, 1), (2, 3), (4, 5), ())
        HERE, LATER = slice(0, CT), slice(CT, NB)
        LATER_T = 11
        SOON, REST = slice(0, (NC - 1) * CT), slice((NC - 1) * CT, NB)
        Q_PART, K_PART = (0, 1, 0), (0, 0, 1)

        def first(b):
            return known(b) and b == 0

        def last(b):
            return known(b) and b == NB - 1

        def slot_after(slot, turn, by):
            return (slot + by) % STACKS, turn + (slot + by) // STACKS

        def exists(b):
            return not known(b) or 0 <= b < NB

        STACKED = 16 * PARTS * HALVES

        def g_slot_used(n, u):
            return n - (GR - 1) if u >= GR else n - (UNITS % GR) + 1 if u < UNITS % GR else n - (UNITS % GR) - GR + 1

        block = ctx.enter_context(nc.Block())

        @block.sync
        def _(sp):
            for c in range(NC):
                cs, bs = slice(c * CH, (c + 1) * CH), slice(c * CT, (c + 1) * CT)
                sp.dma_start(cT[:, :, cs], ctx_t[:, :, cs]).then_inc(ctx_in[c], 16)
                sp.dma_start(xres[:, bs, :], x_t[:, bs, :]).then_inc(x_in[c], 16)
            sp.dma_start(bias[:], bfc.partition_broadcast(P)).then_inc(bias_in, 16)
            sp.dma_start(wfc[:], weight_view(WfcT)).then_inc(wfc_in, 16)
            sp.dma_start(wr_raw[:], weight_view(wr)).then_inc(wr_in, 16)

            def load_stack(b, slot):
                sp.dma_start(qs[slot][0:ROWS, :].bitcast(f32).rearrange("p (g t) -> p g t", t=S),
                             q_dram.rearrange("p g (b t) -> p g b t", t=S)[:, :, bass.ds(b, 1), :]
                             .rearrange("p g b t -> p g (b t)")).then_inc(stack_in[slot], 16)

            def store(c, part):
                for half in range(HALVES):
                    sp.dma_start(q_dram[part * GROUP_ROWS:(part + 1) * GROUP_ROWS, half * GH:(half + 1) * GH,
                                        c * CH:(c + 1) * CH].rearrange("r j t -> j r t"),
                                 qhl[c % QR][:, half, Q_PART[part], :].bitcast(f32)).then_inc(stacked[c], 16)

            def load_row(b, slot):
                sp.wait_ge(row_made, b + 1)
                sp.dma_start(qs[slot][ROWS:ROWS + QUADS, :].bitcast(f32), mrow[slot][:].bitcast(f32))\
                  .then_inc(row_in[slot], 16)

            for c in range(NC):
                if c == NC - 1:
                    sp.wait_ge(fill_made, STACKS)
                    load_row(0, 0)
                sp.wait_ge(q_hi_made, HALVES * (c + 1))
                for part in (0, 2):
                    store(c, part)
                sp.wait_ge(q_lo_made, HALVES * (c + 1))
                store(c, 1)
                if c == 0:
                    sp.wait_ge(stacked[0], STACKED)
                    for b in range(STACKS):
                        load_stack(b, b)

            def sp_batch(b, slot, turn):
                if not first(b):
                    load_row(b, slot)
                if first(b):
                    for c in range(1, NC):
                        sp.wait_ge(stacked[c], STACKED)
                elif exists(b + STACKS - 1):
                    sp.wait_ge(st_psum, PAIRS * b)
                    load_stack(b + STACKS - 1, (slot + STACKS - 1) % STACKS)

            batches(sp, sp_batch)
            def store_out(c):
                bs = bass.ds(c * CT, CT)
                sp.wait_ge(final, 2 * (c + 1))
                sp.dma_start(out_t[:, bs, :], xres[:, bs, :]).then_inc(stored, 16)

            def load_shares(c, es):
                for e in es:
                    wait(sp, prod_done, UNITS * c + SHARED + e + 1 - (SR if e >= SR else SR + SHARED))
                    sp.dma_start(shares[:, e % SR, :], cw_dram[e, :][bass.ds(c * CH, CH)].partition_broadcast(P))\
                      .then_inc(share_in[e % SR], 16)

            def store_shares(c):
                cs = slice(c * CH, (c + 1) * CH)
                sp.wait_ge(cwT_made, c + 1)
                sp.dma_start(cw_dram[:, cs], cwT[:, cs]).then_inc(cw_stored[c], 16)

            store_shares(0)
            sp.wait_ge(cw_stored[0], 16)
            load_shares(0, range(2 * SR))
            for c in range(1, NC):
                store_shares(c)
            load_shares(0, range(2 * SR, E))
            for c in range(1, NC):
                sp.wait_ge(cw_stored[c], 16)
            with sp.Fori(1, NC) as c:
                load_shares(c, range(SR))
                store_out(c - 1)
                load_shares(c, range(SR, E))
            store_out(NC - 1)
            sp.wait_ge(stored, 16 * NC)

        @block.scalar
        def _(act):
            act.dma_start(wk[:], weight_view(WkT)).then_inc(wk_in, 16)
            act.dma_start(wv[:], weight_view(WvT)).then_inc(wv_in, 16)
            act.dma_start(wq[:], weight_view(WqT)).then_inc(wq_in, 16)

            def roots(c, bs):
                act.wait_ge(var_made, c + 1)
                act.activation(root[:, bs], var[:, bs], ACT.Sqrt).then_inc(root_made, 1)

            act.wait_ge(warm_made, 1)
            act.activation(warm[:], warm[:], ACT.Sqrt)
            def high_k(c, half):
                act.wait_ge(k_psum, HALVES * c + half + 1)
                act.activation(kst[0:ROWS, half, c * CH:(c + 1) * CH], psK[:], ACT.Copy).then_inc(k_hi_made, 1)

            def norm_x(c):
                act.wait_ge(rstd_made, c + 1)
                wait(act, xT_psum, c)
                for t in range(CT):
                    b = c * CT + t
                    act.activation(xn[:, t, :], xres[:, b, :], ACT.Identity, bias=shift[:, b:b + 1],
                                   scale=rstd[:, b:b + 1]).then_inc(xn_made, 1)

            def high_w(u):
                act.wait_ge(raw_in[u % 2], 16 * (u // 2 + 1))
                act.activation(Wu[u][:, 0, :], raw[u % 2][:], ACT.Copy).then_inc(w_hi, 1)

            def block_keys(b, slot):
                for quad in range(QUADS - 2, QUADS):
                    ins = act.activation(ks[slot][0:ROWS, quad, :, :], kst[0:ROWS, :, bass.ds(b * S, S)].bitcast(f32),
                                         ACT.Copy, scale=own[0:ROWS, quad:quad + 1])
                ins.then_inc(ks_other_made, 1)

            roots(0, slice(0, CT))
            high_k(0, 0)
            norm_x(0)
            for c in range(NC):
                act.wait_ge(xT_psum, c + 1)
                wait(act, q_psum, 2 * c)
                act.activation(xT[:], psT[:], ACT.Copy).then_inc(xT_made, 1)
                if c + 1 < NC:
                    roots(c + 1, slice((c + 1) * CT, (c + 2) * CT))
                high_k(c, 1)
                if c + 1 < NC:
                    norm_x(c + 1)
                for half in range(HALVES):
                    act.wait_ge(q_psum, 2 * c + half + 1)
                    if half == 0 and c >= QR:
                        act.wait_ge(stacked[c - QR], STACKED)
                    act.activation(qhl[c % QR][:, half, 0, :], psQ[half][:], ACT.Copy).then_inc(q_hi_made, 1)
                if c + 1 < NC:
                    high_k(c + 1, 0)
                for u in CUTS[c]:
                    high_w(u)
                if c == 0:
                    act.wait_ge(own_made, 1)
                    act.wait_ge(k_lo_made, HALVES)
                if c < 2:
                    block_keys(c, c)

            act.activation(warm[:], warm[:], ACT.Exp)
            act.wait_ge(k_lo_made, HALVES * NC)
            def act_oT(b):
                act.wait_ge(oT_psum, b + 1)
                act.activation(OT[:].rearrange("p k t -> p (k t)"), psM[:, 0:D], ACT.Copy).then_inc(oT_made, 1)

            def act_batch(b, slot, turn):
                for p in range(PAIRS):
                    n, r = PAIRS * b + p, p
                    if p == 1 and exists(b + 2):
                        block_keys(b + 2, (slot + 2) % STACKS)
                    act.wait_ge(st_psum, n + 1)
                    wait(act, pv_done, n - PR + 1)
                    act.activation(phi[r][:], psST[p % 2][:], ACT.Exp, scale=SCALE).then_inc(phi_made, 1)
                    wait(act, plo_made, n - PR + 1)
                    act.activation(p32[r][:], psST[p % 2][:], ACT.Exp, scale=SCALE).then_inc(p32_made, 1)
                    if p == 3 and exists(b - 1):
                        act_oT(b - 1)

            batches(act, act_batch, peeled=2)

            def high_x2(c):
                act.wait_ge(x2_psum, c + 1)
                for k in range(KC):
                    act.activation(x2hi[:, k, c * CH:(c + 1) * CH], x2_banks[c % 2][k][:], ACT.Copy)\
                       .then_inc(x2_hi_made, 1)

            def silu(n, u):
                act.wait_ge(up_done, n + 1)
                wait(act, glo_made, n - 1)
                act.activation(h[u % 2][:], psH[u % 2][:], ACT.Silu).then_inc(silu_done, 1)

            def high_g(n, u):
                act.wait_ge(prod_done, n + 1)
                wait(act, down_done, g_slot_used(n, u))
                act.activation(ghi[u % GR][:], h[u % 2][:], ACT.Copy).then_inc(ghi_made, 1)

            roots(NC, SOON)
            high_x2(0)
            act_oT(NB - 1)
            high_x2(1)
            roots(NC + 1, REST)
            high_x2(2)
            def logits_T(c):
                act.wait_ge(logitsT_psum, c + 1)
                act.activation(logitsT[c], logitsT_banks[c][0:2 * E, :], ACT.Copy).then_inc(logitsT_made, 1)

            def exponentials(n, bs):
                act.wait_ge(shifted, n)
                act.activation(pr[:, bs, :], lg[:, bs, :], ACT.Exp).then_inc(exps, 1)

            def shares_T(c):
                act.wait_ge(cwT_psum, c + 1)
                act.activation(cwT[:, c * CH:(c + 1) * CH], psC[c % 2][0:E, :], ACT.Copy).then_inc(cwT_made, 1)

            silu(0, 0)
            high_x2(3)
            logits_T(0)
            act.wait_ge(x1_made, NB)
            high_w(EARLY)
            high_g(0, 0)
            silu(1, 1)
            logits_T(1)
            exponentials(1, HERE)
            logits_T(2)
            high_w(EARLY + 1)
            high_g(1, 1)
            logits_T(3)
            silu(2, 2)
            high_w(EARLY + 2)
            high_g(2, 2)
            silu(3, 3)
            shares_T(0)
            high_w(EARLY + 3)

            def act_y(c):
                act.wait_ge(down_done, UNITS * (c + 1))
                for m in range(KC):
                    act.activation(ysb[m], psY[m][:], ACT.Copy).then_inc(y_made, 1)

            def act_chunk(c):
                for u in range(UNITS):
                    silu(UNITS * c + u, u)
                    high_g(UNITS * c + u, u)
                    if u == 1:
                        act_y(c - 1)

            for u in range(SHARED, UNITS):
                silu(u, u)
                high_g(u - 1, u - 1)
                if EARLY + u < UNITS:
                    if EARLY + u >= UNITS - LATE:
                        act.wait_ge(cwT_psum, NC)
                    high_w(EARLY + u)
                if u == SHARED + 1:
                    exponentials(2, LATER)
                if u == LATER_T:
                    for c in range(1, NC):
                        shares_T(c)
            high_g(UNITS - 1, UNITS - 1)
            with act.Fori(1, NC) as c:
                act_chunk(c)
            act_y(NC - 1)

        @block.gpsimd
        def _(pool):
            pool.memset(ident[:], 0.0).then_inc(ident_zero, 1)
            pool.wait_ge(ident_zero, 1)
            pool.affine_select(out=ident[:], in_=ident[:], compare_op=ALU.not_equal, fill=1.0, base=0,
                               pattern=[[-1, P]], channel_multiplier=1).then_inc(ident_made, 1)

            def load_raw(u):
                wait(pool, w_lo, u - 1)
                pool.dma_start(raw[u % 2][:], W[u]).then_inc(raw_in[u % 2], 16)

            def cut_lo(u):
                pool.wait_ge(w_hi, u + 1)
                pool.tensor_tensor(Wu[u][:, 1, :], raw[u % 2][:], Wu[u][:, 0, :].bitcast(f32), ALU.subtract)\
                    .then_inc(w_lo, 1)
                if u + 2 < UNITS:
                    load_raw(u + 2)

            pool.memset(in_part[:], 1.0).then_inc(part_ones, 1)
            pool.wait_ge(part_ones, 1)
            pool.affine_select(out=in_part[:], in_=in_part[:], compare_op=ALU.is_ge, fill=0.0, base=0,
                               pattern=[[-GROUP_ROWS, PARTS], [-HD, QUADS]], channel_multiplier=1).then_inc(part_ones, 1)
            pool.wait_ge(part_ones, 2)
            pool.affine_select(out=in_part[:], in_=in_part[:], compare_op=ALU.is_ge, fill=0.0, base=HD - 1,
                               pattern=[[GROUP_ROWS, PARTS], [HD, QUADS]], channel_multiplier=-1).then_inc(part_made, 1)
            load_raw(0)
            load_raw(1)
            pool.wait_ge(part_made, 1)
            for slot in range(STACKS):
                rows = ks[slot][ROWS:P, :, :, :].rearrange("p q h t -> p q (h t)")
                pool.memset(ks[slot][ROWS:P, :, :, :].bitcast(f32), 0.0).then_inc(ks_zero, 1)
                pool.memset(qs[slot][ROWS:P, :].bitcast(f32), 0.0).then_inc(fill_made, 1)
                pool.wait_ge(ks_zero, slot + 1)
                pool.wait_ge(fill_made, slot + 1)
                pool.affine_select(out=rows, in_=rows.bitcast(f32), compare_op=ALU.not_equal, fill=-1.0, base=0,
                                   pattern=[[-1, QUADS], [0, HALVES * S]], channel_multiplier=1).then_inc(ks_ready, 1)
                pool.wait_ge(ks_ready, slot + 1)
            pool.wait_ge(bias_in, 16)
            for c in range(NC):
                pool.wait_ge(xn_made, CT * (c + 1))
                here = xres[:, c * CT:(c + 1) * CT, :]
                pool.tensor_tensor(here, here, bias[:].unsqueeze(1).broadcast_to([P, CT, D]), ALU.add)\
                    .then_inc(bias_added, 1)
                for u in CUTS[c]:
                    cut_lo(u)

            def pool_batch(b, slot, turn):
                for p in range(PAIRS - 1 if last(b) else PAIRS):
                    n, r = PAIRS * b + p, p
                    pool.wait_ge(p32_made, n + 1)
                    wait(pool, pv_done, n - PR + 1)
                    pool.tensor_tensor(plo[r][:], p32[r][:], phi[r][:], ALU.subtract).then_inc(plo_made, 1)

            batches(pool, pool_batch)

            pool.wait_ge(x1_made, NB)
            for u in range(EARLY, UNITS):
                cut_lo(u)

        @block.vector
        def _(dve):
            steps = Steps(dve, dve_steps)

            def variances(bs):
                for b in range(bs.start, bs.stop):
                    ins = dve.bn_aggr(mv[:, b, :], stats[:, b, :])
                steps.link(ins)
                dve.tensor_scalar(var[:, bs], mv[:, bs, 1], EPS, None, ALU.add).then_inc(var_made, 1)

            def make_rstd(times, bs):
                dve.wait_ge(root_made, times)
                steps.link(dve.reciprocal(rstd[:, bs], root[:, bs]))
                steps.link(dve.tensor_tensor(newton[:, bs], rstd[:, bs], rstd[:, bs], ALU.mult))
                steps.link(dve.tensor_tensor(newton[:, bs], newton[:, bs], var[:, bs], ALU.mult))
                steps.link(dve.tensor_scalar(newton[:, bs], newton[:, bs], -0.5, 1.5, ALU.mult, ALU.add))
                steps.link(dve.tensor_tensor(rstd[:, bs], rstd[:, bs], newton[:, bs], ALU.mult))
                dve.scalar_tensor_tensor(shift[:, bs], mv[:, bs, 0], -1.0, rstd[:, bs], ALU.mult, ALU.mult)\
                   .then_inc(rstd_made, 1)

            def normed(to, b):
                return dve.tensor_scalar(to, xres[:, b, :], mv[:, b, 0:1], rstd[:, b:b + 1], ALU.subtract, ALU.mult)

            def maximum(b, g, slot):
                dve.wait_ge(s_psum, GROUPS * b + g + 1)
                if g == 0:
                    wait(dve, maxT_psum, b - STACKS + 2)
                dve.tensor_reduce(mx[slot][:, :, g // GH, g % GH], psS[g % 2][:].rearrange("p (q t) -> p q t", q=QUADS),
                                  AX, ALU.max).then_inc(max_made, 1)

            def max_row(b, slot):
                dve.wait_ge(maxT_psum, b + 1)
                dve.tensor_copy(mrow[slot][:], psM[0:HEADS, 0:P]).then_inc(row_made, 1)

            def first_maxima(i):
                for g in (2 * i, 2 * i + 1):
                    maximum(0, g, 0)

            dve.memset(V3[:, :, :, 3 * HD:3 * HD + 1], 1.0)
            dve.memset(warm[:], 1.0).then_inc(warm_made, 1)
            steps.link(dve.memset(minus_hi[:], 0.0))
            dve.memset(minus_hi[2 * GROUP_ROWS:ROWS, :], -1.0)

            def tiles(c):
                return slice(c * CT, (c + 1) * CT)

            def stats_x(c):
                dve.wait_ge(x_in[c], 16)
                for b in range(c * CT, (c + 1) * CT):
                    ins = dve.bn_stats(stats[:, b, :], xres[:, b, :])
                steps.link(ins)
                variances(tiles(c))

            def keys_lo(c, half):
                here = kst[0:ROWS, half, c * CH:(c + 1) * CH]
                dve.wait_ge(k_hi_made, HALVES * c + half + 1)
                dve.scalar_tensor_tensor(here, here.bitcast(f32), minus_hi[0:ROWS, :], psK[:], ALU.mult, ALU.add)\
                   .then_inc(k_lo_made, 1)

            def block_keys(b, slot):
                for quad in range(QUADS - 2):
                    ins = dve.tensor_scalar(ks[slot][0:ROWS, quad, :, :],
                                            kst[0:ROWS, :, bass.ds(b * S, S)].bitcast(f32),
                                            own[0:ROWS, quad:quad + 1], None, ALU.mult)
                ins.then_inc(ks_made, 1)

            def values_cut(c):
                dve.wait_ge(v_psum, c + 1)
                vps = psV[:, 0:CT, :].rearrange("p t (g d) -> p t g d", g=GROUPS)
                part = [V3[:, c * CT:(c + 1) * CT, :, HD * i:HD * (i + 1)] for i in range(3)]
                steps.link(dve.tensor_copy(part[0], vps))
                steps.link(dve.tensor_tensor(vres[:], vps, part[0], ALU.subtract))
                steps.link(dve.tensor_copy(part[1], vres[:]))
                steps.link(dve.tensor_tensor(vres[:], vres[:], part[1], ALU.subtract))
                dve.tensor_copy(part[2], vres[:]).then_inc(v_made, 1)

            def maxima_in(c, i):
                if c == NC - 1:
                    first_maxima(i)

            stats_x(0)
            make_rstd(1, tiles(0))
            dve.wait_ge(part_made, 1)
            dve.tensor_reduce(own[:], in_part[:].rearrange("p s q -> p q s"), AX, ALU.add).then_inc(own_made, 1)
            dve.wait_ge(own_made, 1)
            keys_lo(0, 0)
            for c in range(NC):
                maxima_in(c, 0)
                if c + 1 < NC:
                    stats_x(c + 1)
                maxima_in(c, 1)
                values_cut(c)
                if c + 1 < NC:
                    make_rstd(c + 2, tiles(c + 1))
                maxima_in(c, 2)
                keys_lo(c, 1)
                for half in range(HALVES):
                    dve.wait_ge(q_hi_made, HALVES * c + half + 1)
                    if half == 0 and c >= QR:
                        dve.wait_ge(stacked[c - QR], STACKED)
                    dve.tensor_tensor(qhl[c % QR][:, half, 1, :], psQ[half][:], qhl[c % QR][:, half, 0, :].bitcast(f32),
                                      ALU.subtract).then_inc(q_lo_made, 1)
                    if half == 0:
                        maxima_in(c, 3)
                        if c == NC - 1:
                            max_row(0, 0)
                if c + 1 < NC:
                    keys_lo(c + 1, 0)
                if c == 0:
                    dve.wait_ge(k_lo_made, HALVES)
                if c < 2:
                    block_keys(c, c)

            def combine(b, half):
                dve.wait_ge(pv_done, PAIRS * b + 2 * half + 2)
                wait(dve, half_made, 2 * b + half)
                dve.reciprocal(rden[:], psO[:, :, 3 * HD])
                dve.tensor_reduce(osum[:], psO[:, :, 0:3 * HD].rearrange("p h (s d) -> p h d s", s=3), AX, ALU.add)\
                   .then_inc(o_read, 1)
                dve.wait_ge(o_read, 2 * b + half + 1)
                if half == 0:
                    wait(dve, oT_psum, b)
                dve.tensor_tensor(O[:, half * P:(half + 1) * P].rearrange("p (h d) -> p h d", d=HD), osum[:],
                                  rden[:].unsqueeze(2).broadcast_to([P, HEADS // 2, HD]), ALU.mult)\
                   .then_inc(half_made, 1)

            def x1_tile(b):
                return xres[:, bass.ds(b, 1), :].rearrange("p b d -> p (b d)")

            def residual(b):
                dve.wait_ge(fc_done, b + 1)
                dve.tensor_tensor(x1_tile(b), psM[:, D:2 * D], x1_tile(b), ALU.add).then_inc(x1_made, 1)

            def x1_stats(b):
                dve.wait_ge(x1_made, b + 1)
                return dve.bn_stats(stats[:, bass.ds(b, 1), :].rearrange("p b s -> p (b s)"), x1_tile(b))

            def dve_batch(b, slot, turn):
                one_on, two_on = ((slot + i) % STACKS for i in (1, 2))
                if exists(b + 1):
                    maximum(b + 1, 3, one_on)
                if exists(b - 1):
                    combine(b - 1, 0)
                if exists(b + 1):
                    for g in (4, 5, 6, 7):
                        maximum(b + 1, g, one_on)
                if exists(b + 2):
                    wait(dve, st_psum, PAIRS * (b - 1))
                    block_keys(b + 2, two_on)
                if exists(b + 1):
                    max_row(b + 1, one_on)
                if exists(b - 2):
                    residual(b - 2)
                if exists(b - 1):
                    combine(b - 1, 1)
                if exists(b + 2):
                    for g in (0, 1):
                        maximum(b + 2, g, two_on)
                if exists(b + 2):
                    maximum(b + 2, 2, two_on)
                if exists(b - 2):
                    x1_stats(b - 2)

            for g in range(3):
                maximum(1, g, 1)
            dve.wait_ge(bias_added, NC)
            batches(dve, dve_batch, peeled=2)
            def products(c, u):
                hu, n = h[u % 2][:], UNITS * c + u
                dve.wait_ge(silu_done, n + 1)
                dve.wait_ge(gate_done, n + 1)
                if u < SHARED:
                    dve.scalar_tensor_tensor(hu, hu, 1.0 / (TOP + 1), psG[u % 2][:], ALU.mult, ALU.mult)\
                       .then_inc(prod_done, 1)
                else:
                    steps.link(dve.tensor_tensor(hu, hu, psG[u % 2][:], ALU.mult))
                    e = u - SHARED
                    dve.wait_ge(share_in[e % SR], 16 * (E // SR * c + e // SR + 1))
                    dve.tensor_tensor(hu, hu, shares[:, e % SR, :], ALU.mult).then_inc(prod_done, 1)

            def low_g(n, u):
                dve.wait_ge(ghi_made, n + 1)
                wait(dve, down_done, g_slot_used(n, u))
                dve.tensor_tensor(glo[u % GR][:], h[u % 2][:], ghi[u % GR][:].bitcast(f32), ALU.subtract)\
                   .then_inc(glo_made, 1)

            def norm_x2(c):
                wait(dve, x2_psum, c - 1)
                for t in range(CT):
                    normed(xn2[c % 2][:, t, :], c * CT + t).then_inc(xn_made, 1)

            def low_x2(c):
                for k in range(KC):
                    dve.wait_ge(x2_hi_made, KC * c + k + 1)
                    here = slice(c * CH, (c + 1) * CH)
                    dve.tensor_tensor(x2lo[:, k, here], x2_banks[c % 2][k][:], x2hi[:, k, here].bitcast(f32),
                                      ALU.subtract).then_inc(x2_lo_made, 1)

            variances(SOON)
            combine(NB - 1, 0)
            dve.wait_ge(p32_made, PAIRS * NB)
            dve.wait_ge(pv_done, PAIRS * NB - PR)
            dve.tensor_tensor(plo[PAIRS - 1][:], p32[PAIRS - 1][:], phi[PAIRS - 1][:], ALU.subtract)\
               .then_inc(last_plo_made, 1)
            make_rstd(NC + 1, SOON)
            norm_x2(0)
            residual(NB - 2)
            combine(NB - 1, 1)
            norm_x2(1)
            low_x2(0)
            residual(NB - 1)
            x1_stats(NB - 2)
            steps.link(x1_stats(NB - 1))
            variances(REST)
            norm_x2(2)
            low_x2(1)
            dve.wait_ge(wr_in, 16)
            steps.link(dve.tensor_copy(wr_cut[:, :, 0, :], wr_raw[:]))
            dve.tensor_tensor(wr_cut[:, :, 1, :], wr_raw[:], wr_cut[:, :, 0, :].bitcast(f32), ALU.subtract)\
               .then_inc(wr_made, 1)
            make_rstd(NC + 2, REST)
            norm_x2(3)
            low_x2(2)
            products(0, 0)
            def like(bs):
                return [P, bs.stop - bs.start, E]

            def shifted_logits(n, bs, bank):
                dve.wait_ge(logits, n)
                lps = bank[:, 0:2 * E * (bs.stop - bs.start)].rearrange("p (b a e) -> p b a e", a=2, e=E)
                steps.link(dve.tensor_copy(lg[:, bs, :], lps[:, :, 0, :]))
                steps.link(dve.tensor_tensor(lg[:, bs, :], lg[:, bs, :], lps[:, :, 1, :], ALU.add))
                steps.link(dve.tensor_reduce(one[:, bs, 0], lg[:, bs, :], AX, ALU.max))
                dve.tensor_tensor(lg[:, bs, :], lg[:, bs, :], one[:, bs, :].broadcast_to(like(bs)), ALU.subtract)\
                   .then_inc(shifted, 1)

            def probabilities(n, bs):
                dve.wait_ge(exps, n)
                steps.link(dve.tensor_reduce(one[:, bs, 0], pr[:, bs, :], AX, ALU.add))
                steps.link(dve.reciprocal(one[:, bs, :], one[:, bs, :]))
                steps.link(dve.tensor_tensor(pr[:, bs, :], pr[:, bs, :], one[:, bs, :].broadcast_to(like(bs)), ALU.mult))

            def largest(bs):
                for b in range(bs.start, bs.stop):
                    ins = dve.max(top8[:, b, :], pr[:, b, :])
                steps.link(ins)
                fourth = top8[:, bs, TOP - 1:TOP].broadcast_to(like(bs))
                dve.tensor_tensor(above[:, bs, :], pr[:, bs, :], fourth, ALU.is_gt)
                steps.link(dve.tensor_tensor(tie[:, bs, :], pr[:, bs, :], fourth, ALU.is_equal))
                steps.link(dve.tensor_reduce(one[:, bs, 0], above[:, bs, :], AX, ALU.add))

            def chosen(bs):
                src = tie
                for i in range(4):
                    dst, step = rank[i % 2], 1 << i
                    dve.tensor_copy(dst[:, bs, 0:step], src[:, bs, 0:step])
                    steps.link(dve.tensor_tensor(dst[:, bs, step:], src[:, bs, step:], src[:, bs, 0:E - step], ALU.add))
                    src = dst
                steps.link(dve.tensor_tensor(rank[0][:, bs, :], src[:, bs, :], one[:, bs, :].broadcast_to(like(bs)),
                                             ALU.add))
                steps.link(dve.scalar_tensor_tensor(rank[1][:, bs, :], rank[0][:, bs, :], float(TOP), tie[:, bs, :],
                                                    ALU.is_le, ALU.mult))
                steps.link(dve.tensor_tensor(rank[0][:, bs, :], rank[1][:, bs, :], above[:, bs, :], ALU.add))

            def expert_shares(bs):
                steps.link(dve.tensor_tensor(lg[:, bs, :], rank[0][:, bs, :], pr[:, bs, :], ALU.mult))
                steps.link(dve.tensor_reduce(one[:, bs, 0], lg[:, bs, :], AX, ALU.add))
                steps.link(dve.reciprocal(one[:, bs, :], one[:, bs, :]))
                steps.link(dve.tensor_scalar(one[:, bs, :], one[:, bs, :], TOP / (TOP + 1.0), None, ALU.mult))
                dve.tensor_tensor(cw[:, bs, :], lg[:, bs, :], one[:, bs, :].broadcast_to(like(bs)), ALU.mult)\
                   .then_inc(cw_made, 1)

            low_x2(3)
            shifted_logits(1, HERE, psY1)
            low_g(0, 0)
            products(0, 1)
            probabilities(1, HERE)
            largest(HERE)
            low_g(1, 1)
            chosen(HERE)
            expert_shares(HERE)
            products(0, 2)
            low_g(2, 2)

            def add_y(c):
                dve.wait_ge(yT_psum, c + 1)
                for i in range(2):
                    here = xres[:, bass.ds(c * CT + 2 * i, 2), :].rearrange("p b d -> p (b d)")
                    dve.tensor_tensor(here, psC[i][:], here, ALU.add).then_inc(final, 1)

            products(0, SHARED - 1)
            for u in range(SHARED, UNITS):
                products(0, u)
                low_g(u - 1, u - 1)
                if u == 4:
                    shifted_logits(2, LATER, psC1)
                elif u == 6:
                    probabilities(2, LATER)
                elif u == 7:
                    largest(LATER)
                elif u == 9:
                    chosen(LATER)
                elif u == 10:
                    expert_shares(LATER)
            low_g(UNITS - 1, UNITS - 1)
            base = steps.n
            with dve.Fori(1, NC) as c:
                steps.n = base + E * (c - 1)
                for u in range(UNITS):
                    products(c, u)
                    low_g(UNITS * c + u, u)
                    if u == 3:
                        add_y(c - 1)
            add_y(NC - 1)

        @block.tensor
        def _(pe):
            mm = pe.matmul

            def scores(b, g, slot, turn):
                if g == 0:
                    pe.wait_ge(stack_in[slot], 16 * (turn + 1))
                    pe.wait_ge(ks_made, b + 1)
                    pe.wait_ge(ks_other_made, b + 1)
                    if known(b) and b == 0:
                        pe.wait_ge(ks_ready, STACKS)
                wait(pe, max_made, GROUPS * b + g - 1)
                mm(psS[g % 2][:], qs[slot][0:ROWS, g * S:(g + 1) * S], ks[slot][0:ROWS, :, g // GH, :],
                   start=True, stop=True).then_inc(s_psum, 1)

            def maxima_T(b, slot):
                pe.wait_ge(max_made, GROUPS * (b + 1))
                pe.transpose(psM[0:HEADS, 0:P], mx[slot][:].rearrange("p q h j -> p (q h j)"), ident[:]).then_inc(maxT_psum, 1)

            def keys(c, half):
                wait(pe, k_lo_made, HALVES * c + half)
                for k in range(KC):
                    ins = mm(psK[:], wk[:, k, half * ROWS:(half + 1) * ROWS], cT[:, k, c * CH:(c + 1) * CH],
                             start=k == 0, stop=k == KC - 1)
                ins.then_inc(k_psum, 1)

            def scores_in(c, i):
                if c == NC - 1:
                    for g in (2 * i, 2 * i + 1):
                        scores(0, g, 0, 0)

            def queries(c, half):
                wait(pe, q_lo_made, HALVES * (c - 1) + half + 1)
                for k in range(KC):
                    ins = mm(psQ[half][:], wq[:, k, half * P:(half + 1) * P], xT[:, k, :],
                             start=k == 0, stop=k == KC - 1)
                ins.then_inc(q_psum, 1)

            def x_turned(c):
                if c == 0:
                    pe.wait_ge(ident_made, 1)
                wait(pe, xT_made, c)
                for t in range(CT):
                    pe.wait_ge(xn_made, c * CT + t + 1)
                    for k in range(KC):
                        ins = pe.transpose(psT[:, k, t * P:(t + 1) * P], xn[:, t, k * P:(k + 1) * P], ident[:])
                ins.then_inc(xT_psum, 1)

            def values_of(c):
                if c == 0:
                    pe.wait_ge(wv_in, 16)
                wait(pe, v_made, c)
                for t in range(CT):
                    for k in range(KC):
                        ins = mm(psV[:, t, :], cT[:, k, (c * CT + t) * P:(c * CT + t + 1) * P], wv[:, k, :],
                                 start=k == 0, stop=k == KC - 1)
                ins.then_inc(v_psum, 1)

            for c in range(NC):
                if c == 0:
                    pe.wait_ge(wk_in, 16)
                pe.wait_ge(ctx_in[c], 16)
                keys(c, 0)
                if c == 0:
                    values_of(c)
                x_turned(c)
                scores_in(c, 0)
                if c > 0:
                    values_of(c)
                scores_in(c, 1)
                keys(c, 1)
                scores_in(c, 2)
                if c == 0:
                    pe.wait_ge(wq_in, 16)
                pe.wait_ge(xT_made, c + 1)
                queries(c, 0)
                scores_in(c, 3)
                queries(c, 1)
            pe.wait_ge(v_made, NC)
            maxima_T(0, 0)

            def scores_T(b, p, slot, turn):
                wait(pe, p32_made, PAIRS * b + p - 1)
                if p == 0:
                    pe.wait_ge(row_in[slot], 16 * (turn + 1))
                for i in range(2):
                    g = 2 * p + i
                    half = g // QUADS
                    ins = mm(psST[p % 2][:, i * GH * S:(i + 1) * GH * S], ks[slot][:, g % QUADS, half, :],
                             qs[slot][:, half * GH * S:(half + 1) * GH * S], start=True, stop=True)
                ins.then_inc(st_psum, 1)

            def values(b, p):
                r = p
                if p % 2 == 0:
                    wait(pe, o_read, 2 * b + p // 2)
                pe.wait_ge(phi_made, PAIRS * b + p + 1)
                if last(b) and p == PAIRS - 1:
                    pe.wait_ge(last_plo_made, 1)
                else:
                    pe.wait_ge(plo_made, PAIRS * b + p + 1)
                for i in range(2 * GH):
                    g = 2 * p + i // GH
                    v = V3[:, bass.ds(b, 1), g, 0:3 * HD + 1].rearrange("p b d -> p (b d)")
                    to = psO[:, (p % 2) * 2 * GH + i, 0:3 * HD + 1]
                    mm(to, phi[r][:, i * S:(i + 1) * S], v, start=True, stop=False)
                    ins = mm(to, plo[r][:, i * S:(i + 1) * S], v, start=False, stop=True)
                ins.then_inc(pv_done, 1)

            def transpose_O(b):
                pe.wait_ge(half_made, 2 * (b + 1))
                pe.wait_ge(row_made, min(b + 3, NB) if known(b) else b + 3)
                for k in range(KC):
                    ins = pe.transpose(psM[:, k * P:(k + 1) * P], O[:, k * P:(k + 1) * P], ident[:])
                ins.then_inc(oT_psum, 1)

            def project(b):
                pe.wait_ge(oT_made, b + 1)
                for k in range(KC):
                    ins = mm(psM[:, D:2 * D], OT[:, k, :], wfc[:, k, :], start=k == 0, stop=k == KC - 1)
                ins.then_inc(fc_done, 1)

            def pe_batch(b, slot, turn):
                one_on, two_on = slot_after(slot, turn, 1), slot_after(slot, turn, 2)
                scores_T(b, 0, slot, turn)
                if exists(b + 1):
                    scores(b + 1, 3, *one_on)
                if exists(b - 1):
                    values(b - 1, 1)
                if exists(b - 2):
                    project(b - 2)
                if exists(b + 1):
                    scores(b + 1, 4, *one_on)
                    scores(b + 1, 5, *one_on)
                scores_T(b, 1, slot, turn)
                if exists(b - 1):
                    values(b - 1, 2)
                if exists(b + 1):
                    scores(b + 1, 6, *one_on)
                    scores(b + 1, 7, *one_on)
                scores_T(b, 2, slot, turn)
                if exists(b - 1):
                    values(b - 1, 3)
                if exists(b + 1):
                    maxima_T(b + 1, one_on[0])
                scores_T(b, 3, slot, turn)
                if exists(b + 2):
                    scores(b + 2, 0, *two_on)
                    scores(b + 2, 1, *two_on)
                values(b, 0)
                if exists(b - 1):
                    transpose_O(b - 1)
                if exists(b + 2):
                    scores(b + 2, 2, *two_on)

            for g in range(3):
                scores(1, g, 1, 0)
            pe.wait_ge(xT_made, NC)
            pe.wait_ge(k_lo_made, HALVES * NC)
            pe.wait_ge(q_lo_made, HALVES * NC)
            pe.wait_ge(wfc_in, 16)
            batches(pe, pe_batch, peeled=2)

            def transpose_x2(c):
                wait(pe, x2_lo_made, KC * (c - 1))
                if c == 1:
                    pe.wait_ge(x1_made, NB)
                for t in range(CT):
                    pe.wait_ge(xn_made, NB + c * CT + t + 1)
                    for k in range(KC):
                        ins = pe.transpose(x2_banks[c % 2][k][:, t * P:(t + 1) * P],
                                           xn2[c % 2][:, t, k * P:(k + 1) * P], ident[:])
                ins.then_inc(x2_psum, 1)

            def logits_of(c):
                if c == 0:
                    pe.wait_ge(wr_made, 1)
                pe.wait_ge(x2_lo_made, KC * (NC - 1 if c == 0 else NC))
                if c == NC - 1:
                    pe.wait_ge(logitsT_made, c - 1)
                i = 0
                for k in range(KC):
                    for xs in (x2hi, x2lo):
                        ins = mm(logitsT_banks[c][0:2 * E, :], wr_cut[:, k, :, :].rearrange("p a e -> p (a e)"),
                                 xs[:, k, c * CH:(c + 1) * CH], start=i == 0, stop=i == 2 * KC - 1)
                        i += 1
                ins.then_inc(logitsT_psum, 1)

            def turn_logits(cs, bank):
                pe.wait_ge(logitsT_made, cs[-1] + 1)
                for i, b in enumerate(range(cs[0] * CT, (cs[-1] + 1) * CT)):
                    ins = pe.transpose(bank[:, 2 * i * E:2 * (i + 1) * E],
                                       logitsT[b // CT][:, (b % CT) * P:(b % CT + 1) * P], ident[0:2 * E, 0:2 * E])
                ins.then_inc(logits, 1)

            def cut_products(to, w, col, c):
                i = 0
                for k in range(KC):
                    at = w[:, 0, col + k * P:col + (k + 1) * P], w[:, 1, col + k * P:col + (k + 1) * P]
                    for ws, xv in ((at[0], x2hi), (at[1], x2hi), (at[0], x2lo)):
                        ins = mm(to, ws, xv[:, k, bass.ds(c * CH, CH)], start=i == 0, stop=i == 3 * KC - 1)
                        i += 1
                return ins

            def up(c, u):
                n = UNITS * c + u
                pe.wait_ge(w_lo, u + 1)
                wait(pe, silu_done, n - 1)
                cut_products(psH[u % 2][:], Wu[u], 0, c).then_inc(up_done, 1)
                wait(pe, prod_done, n - 1)
                cut_products(psG[u % 2][:], Wu[u], D, c).then_inc(gate_done, 1)

            def down(c, u):
                if u == 0:
                    wait(pe, y_made, KC * c)
                pe.wait_ge(glo_made, UNITS * c + u + 1)
                for m in range(KC):
                    at = 2 * D + m * P
                    i = 0
                    for wp, gs in ((0, ghi), (1, ghi), (0, glo)):
                        ins = mm(psY[m][:], Wu[u][:, wp, at:at + P], gs[u % GR][:], start=u == 0 and i == 0,
                                 stop=u == UNITS - 1 and i == 2)
                        i += 1
                ins.then_inc(down_done, 1)

            def transpose_y(c):
                pe.wait_ge(y_made, KC * (c + 1))
                pe.wait_ge(prod_done, UNITS * (c + 1))
                for t in range(CT):
                    for m in range(KC):
                        ins = pe.transpose(psC[t // 2][:, ((t % 2) * KC + m) * P:((t % 2) * KC + m + 1) * P],
                                           ysb[m][:, t * P:(t + 1) * P], ident[:])
                ins.then_inc(yT_psum, 1)

            def pe_chunk(c, start=0):
                for u in range(start, UNITS):
                    up(c, u)
                    if u < 2:
                        down(c - 1, UNITS - 2 + u)
                    else:
                        if u == 2 and not first(c):
                            transpose_y(c - 1)
                        down(c, u - 2)
                    if u == LATER_T and first(c):
                        weights_T(2, range(1, NC))

            def weights_T(n, cs):
                pe.wait_ge(cw_made, n)
                for c in cs:
                    wait(pe, cwT_made, c - 1)
                    for t in range(CT):
                        ins = pe.transpose(psC[c % 2][0:E, t * P:(t + 1) * P], cw[:, c * CT + t, :], ident[:])
                    ins.then_inc(cwT_psum, 1)

            values(NB - 1, 1)
            project(NB - 2)
            values(NB - 1, 2)
            values(NB - 1, 3)
            transpose_x2(0)
            transpose_O(NB - 1)
            project(NB - 1)
            pe.wait_ge(x2_lo_made, KC)
            transpose_x2(1)
            up(0, 0)
            transpose_x2(2)
            up(0, 1)
            transpose_x2(3)
            logits_of(0)
            turn_logits([0], psY1)
            logits_of(1)
            logits_of(2)
            up(0, 2)
            logits_of(3)
            pe.wait_ge(shifted, 1)
            down(0, 0)
            turn_logits(range(1, NC), psC1)
            up(0, 3)
            weights_T(1, [0])
            down(0, 1)
            pe_chunk(0, 4)
            with pe.Fori(1, NC) as c:
                pe_chunk(c)
            down(NC - 1, UNITS - 2)
            down(NC - 1, UNITS - 1)
            transpose_y(NC - 1)


def kernel(x, ctx_2048, L0_xattn_Wq, L0_xattn_Wk, L0_xattn_Wv, L0_xattn_Wfc, L0_xattn_bfc, L0_ffn_w_router,
           L0_ffn_we1, L0_ffn_we3, L0_ffn_we2, L0_ffn_ws1, L0_ffn_ws3, L0_ffn_ws2):
    import numpy as np
    import concourse.bacc as bacc
    from concourse.bass_utils import run_bass_kernel_spmd

    def halves_of(w):
        return np.concatenate([w[..., k * P:(k + 1) * P, :] for k in range(KC)], axis=-1)

    def columns(w):
        return np.stack([w[:, u * P:(u + 1) * P] for u in range(SHARED)])

    a = {k: np.asarray(v) for k, v in dict(
        x=x, ctx=ctx_2048, Wq=L0_xattn_Wq, Wk=L0_xattn_Wk, Wv=L0_xattn_Wv, Wfc=L0_xattn_Wfc, bfc=L0_xattn_bfc,
        wr=L0_ffn_w_router, we1=L0_ffn_we1, we3=L0_ffn_we3, we2=L0_ffn_we2, ws1=L0_ffn_ws1, ws3=L0_ffn_ws3,
        ws2=L0_ffn_ws2).items()}
    wq = a["Wq"].reshape(HALVES, QUADS, GH, HD, D).transpose(0, 2, 1, 3, 4).reshape(D, D)
    shared = np.concatenate([halves_of(columns(a["ws1"])), halves_of(columns(a["ws3"])),
                             a["ws2"].reshape(SHARED, P, D)], axis=-1)
    experts = np.concatenate([halves_of(a["we1"]), halves_of(a["we3"]), a["we2"]], axis=-1)
    wk = np.repeat(a["Wk"].reshape(HALVES, 1, GROUP_ROWS, D), PARTS, axis=1).reshape(HALVES * ROWS, D)
    arrays = {
        "x": a["x"].reshape(T, D), "ctxT": a["ctx"].reshape(T, D).T, "WqT": wq.T, "WkT": wk.T, "WvT": a["Wv"].T,
        "WfcT": a["Wfc"].T, "bfc": a["bfc"], "wr": a["wr"], "W": np.concatenate([shared, experts]),
    }
    nc = bacc.Bacc("TRN2", target_bir_lowering=False, num_devices=1)
    args, given = {}, {}
    for name, v in arrays.items():
        v = np.ascontiguousarray(v)
        given[f"in_{name}"] = v
        args[name] = nc.dram_tensor(f"in_{name}", v.shape, mybir.dt.from_np(v.dtype), kind="ExternalInput").ap()
    out = nc.dram_tensor("out_0", (T, D), mybir.dt.float32, kind="ExternalOutput").ap()
    build(nc, out=out, **args)
    got = run_bass_kernel_spmd(nc, [given], core_ids=[0])
    return got.results[0]["out_0"].reshape(NB, S, D)
```
